# Optimizing a Trainium2 kernel written in Bass

```python
import numpy as np
import jax
import jax.numpy as jnp

def _softmax(x, axis=-1):
    return jax.nn.softmax(x, axis=axis)

def _gelu(x):
    return jax.nn.gelu(x, approximate=True)

def _silu(x):
    return jax.nn.silu(x)

def _sigmoid(x):
    return jax.nn.sigmoid(x)

def _layernorm(x, axis=-1, eps=1e-05):
    m = jnp.mean(x, axis=axis, keepdims=True)
    v = jnp.var(x, axis=axis, keepdims=True)
    return (x - m) / jnp.sqrt(v + eps)

def _scatter_add(tgt, idx, src, axis=0):
    return tgt.at[idx].add(src)

def _segment_sum(src, seg, n):
    return jax.ops.segment_sum(src, seg, n)
kernel_name = 'mk_gnn_preln_d1_gnn_r8_c736ee'

def setup_inputs(seed: int=0):
    np.random.seed(seed)
    _w = jnp.asarray

    def _rec_inputs():
        import jax
        import jax.numpy as jnp
        _gk = jax.random.key(seed)
        x = -1.686e-05 + 1 * jax.random.normal(jax.random.fold_in(_gk, 1), (6250, 160), jnp.float32)
        _s = jax.random.randint(jax.random.fold_in(_gk, 2), (100000,), 0, 6250, jnp.int32)
        _d = jax.random.randint(jax.random.fold_in(_gk, 3), (100000,), 0, 6250, jnp.int32)
        _loop = jnp.arange(6250, dtype=jnp.int32)
        src = jnp.concatenate([_s, _d, _loop])
        dst = jnp.concatenate([_d, _s, _loop])
        _o = jnp.argsort(dst, stable=True)
        src = src[_o]
        dst = dst[_o]
        edge_attr_4 = -0.000107899 + 1.00008 * jax.random.normal(jax.random.fold_in(_gk, 11), (206250, 4), jnp.float32)
        return (x, src, dst, edge_attr_4)
    x, src, dst, edge_attr_4 = _rec_inputs()

    def _L0_gnn_setup():
        import jax, jax.numpy as jnp
        import numpy as np
        N, E = (6250, 100000)
        MUL0, MUL1 = (64, 32)
        D = MUL0 + 3 * MUL1
        INV3 = float(1.0 / np.sqrt(3.0))
        INV6 = float(1.0 / np.sqrt(6.0))
        C0 = float(1.0 / np.sqrt(MUL0 + MUL1))
        C1 = float(np.sqrt(3.0 / (MUL0 + 2 * MUL1)))
        LIN_S = float(1.0 / np.sqrt(MUL0))
        LIN_V = float(1.0 / np.sqrt(MUL1))
        key = jax.random.key(seed)
        ks = jax.random.split(key, 10)
        x = jax.random.normal(ks[0], (N, D), dtype=jnp.float32)
        sh = jax.random.normal(ks[1], (E, 4), dtype=jnp.float32)
        edge_index = jax.random.randint(ks[2], (2, E), 0, N, dtype=jnp.int64)
        W1 = jax.random.normal(ks[3], (MUL0, MUL0), dtype=jnp.float32)
        W2 = jax.random.normal(ks[4], (MUL1, MUL0), dtype=jnp.float32)
        W3 = jax.random.normal(ks[5], (MUL0, MUL1), dtype=jnp.float32)
        W4 = jax.random.normal(ks[6], (MUL1, MUL1), dtype=jnp.float32)
        W5 = jax.random.normal(ks[7], (MUL1, MUL1), dtype=jnp.float32)
        Ws = jax.random.normal(ks[8], (MUL0, MUL0), dtype=jnp.float32)
        Wv = jax.random.normal(ks[9], (MUL1, MUL1), dtype=jnp.float32)
        return {'x': x, 'sh': sh, 'W1': W1, 'W2': W2, 'W3': W3, 'W4': W4, 'W5': W5, 'Ws': Ws, 'Wv': Wv, 'edge_index': edge_index}
    _L0_gnn_all = _L0_gnn_setup()
    _L0_gnn_in = {k: v for k, v in _L0_gnn_all.items() if k in ('W1', 'W2', 'W3', 'W4', 'W5', 'Ws', 'Wv')}
    del _L0_gnn_all
    return {'x': x, 'src': src, 'dst': dst, 'edge_attr_4': edge_attr_4, 'L0_gnn_W1': _L0_gnn_in['W1'], 'L0_gnn_W2': _L0_gnn_in['W2'], 'L0_gnn_W3': _L0_gnn_in['W3'], 'L0_gnn_W4': _L0_gnn_in['W4'], 'L0_gnn_W5': _L0_gnn_in['W5'], 'L0_gnn_Ws': _L0_gnn_in['Ws'], 'L0_gnn_Wv': _L0_gnn_in['Wv']}

def reference(x, src, dst, edge_attr_4, L0_gnn_W1, L0_gnn_W2, L0_gnn_W3, L0_gnn_W4, L0_gnn_W5, L0_gnn_Ws, L0_gnn_Wv):
    import jax
    import jax.numpy as jnp

    def _L0_gnn_ref(x, sh, W1, W2, W3, W4, W5, Ws, Wv, edge_index):
        import jax, jax.numpy as jnp
        import numpy as np
        N, E = (6250, 100000)
        MUL0, MUL1 = (64, 32)
        D = MUL0 + 3 * MUL1
        INV3 = float(1.0 / np.sqrt(3.0))
        INV6 = float(1.0 / np.sqrt(6.0))
        C0 = float(1.0 / np.sqrt(MUL0 + MUL1))
        C1 = float(np.sqrt(3.0 / (MUL0 + 2 * MUL1)))
        LIN_S = float(1.0 / np.sqrt(MUL0))
        LIN_V = float(1.0 / np.sqrt(MUL1))
        n = x.shape[0]
        src, dst = (edge_index[0], edge_index[1])
        s = x[:, :MUL0]
        v = x[:, MUL0:].reshape(n, MUL1, 3)
        ss, vv = (s[src], v[src])
        e0 = sh[:, 0:1]
        e1 = sh[:, 1:4]
        dot = jnp.einsum('eui,ei->eu', vv, e1)
        out0 = C0 * (ss * e0 @ W1 + dot * INV3 @ W2)
        p3 = (ss @ W3)[:, :, None] * e1[:, None, :] * INV3
        p4 = jnp.einsum('eui,uw->ewi', vv * e0[:, :, None], W4) * INV3
        p5 = jnp.einsum('eui,uw->ewi', jnp.cross(vv, e1[:, None, :]), W5) * INV6
        out1 = C1 * (p3 + p4 + p5)
        m = jnp.concatenate([out0, out1.reshape(-1, 3 * MUL1)], axis=1)
        m_agg = jax.ops.segment_sum(m, dst, num_segments=n)
        hs = m_agg[:, :MUL0] @ Ws * LIN_S
        hv = jnp.einsum('nui,uw->nwi', m_agg[:, MUL0:].reshape(n, MUL1, 3), Wv) * LIN_V
        h = jnp.concatenate([hs, hv.reshape(n, 3 * MUL1)], axis=1)
        return x + jax.nn.relu(h)
    edge_index = jnp.stack([src, dst])
    h = jnp.maximum(_layernorm(x, axis=-1), 0.0)
    x = x + _L0_gnn_ref(h, edge_attr_4, L0_gnn_W1, L0_gnn_W2, L0_gnn_W3, L0_gnn_W4, L0_gnn_W5, L0_gnn_Ws, L0_gnn_Wv, edge_index)
    return x

_drawn_inputs = setup_inputs


def setup_inputs(seed=0):
    import zlib

    import numpy as np

    out = dict(_drawn_inputs(seed))
    spreads = {}
    factors = {}
    for name, (base, spread) in spreads.items():
        noise = np.random.default_rng([zlib.crc32(name.encode()), seed]).standard_normal(out[name].shape)
        drawn = base * np.exp(spread * noise) if base else spread * noise
        out[name] = jnp.asarray(drawn.astype(out[name].dtype))
    for name, factor in factors.items():
        out[name] = (out[name] * factor).astype(out[name].dtype)
    return out
```

```python
from contextlib import ExitStack

import concourse.bass as bass
from concourse import mybir

F32 = mybir.dt.float32
I32 = mybir.dt.int32
ALU = mybir.AluOpType
ACT = mybir.ActivationFunctionType
AX_X = mybir.AxisListType.X

NODES = 6250
MUL0, MUL1 = 64, 32
D = MUL0 + 3 * MUL1
EDGES = 206250
EPS = 1e-5

C0 = (MUL0 + MUL1) ** -0.5
C1 = (3.0 / (MUL0 + 2 * MUL1)) ** 0.5
INV3 = 3.0 ** -0.5
INV6 = 6.0 ** -0.5
LIN_S = MUL0 ** -0.5
LIN_V = MUL1 ** -0.5

P = 128
TPG = 4
W = 32
GROUPS = -(-EDGES // (P * TPG))
TILES = GROUPS * TPG
RING = 8
HALF = RING // 2
TURNS = (GROUPS - 1) // RING
TAIL = GROUPS - TURNS * RING
LEAD = 2
assert LEAD <= TAIL <= HALF

NP = 125
PER = NODES // NP
CHUNKS = 5
CH = PER // CHUNKS
H_BUFS = CHUNKS - 1
BLK = 3
WINDOWS = -(-NODES // W)
COLS = WINDOWS * W + W
F1, F2 = P, D - P


def gnn_kernel(nc: bass.Bass, x, src, dst, sh, w1t, w2t, w3t, w4t, w5t, ws, wv, table, out):
    x_v = x.rearrange("(p j) d -> p (j d)", p=NP)
    table_v = table.rearrange("(p j) d -> p (j d)", p=NP)
    out_v = out.rearrange("(p j) d -> p (j d)", p=NP)

    with ExitStack() as ctx:
        def sb(name, shape, dt=F32):
            return ctx.enter_context(nc.sbuf_tensor(name, shape, dt))

        def ps(name, shape):
            return ctx.enter_context(nc.psum_tensor(name, shape, F32))

        def sem(name):
            return ctx.enter_context(nc.semaphore(name))

        xh = sb("xh", [NP, PER, D])
        h = sb("h", [NP, H_BUFS, CH, D])
        stats = sb("stats", [NP, PER, 6])
        mv = sb("mv", [NP, PER, 2])
        std = sb("std", [NP, PER])
        rstd = sb("rstd", [NP, PER])
        shift = sb("shift", [NP, PER])
        eps_t = sb("eps_t", [P, 1])
        acc1 = sb("acc1", [F1, COLS])
        acc2 = sb("acc2", [F2, COLS])
        dst_i = sb("dst_i", [P, TILES], I32)
        rel = sb("rel", [P, TILES])
        sh_sb = sb("sh_sb", [P, TILES, 4])
        idx = [sb(f"idx{k}", [P, HALF * TPG], I32) for k in range(2)]
        base_f = sb("base_f", [1, GROUPS])
        base_i = sb("base_i", [1, GROUPS], I32)
        outside = sb("outside", [P, TILES])
        group_out = sb("group_out", [P, GROUPS])
        n_out = sb("n_out", [1, GROUPS], I32)
        n_out_f = sb("n_out_f", [1, 1])
        n_out_all = sb("n_out_all", [1, 1], I32)
        rows = sb("rows", [P, RING, TPG, D])
        onehot = sb("onehot", [P, 2, TPG, W])
        scat = sb("scat", [P, 4, TPG, 4, W])
        agg1 = sb("agg1", [F1, 2, 4, W])
        agg2 = sb("agg2", [P, 2, W])
        iota_i = sb("iota_i", [P, W], I32)
        iota_w = sb("iota_w", [P, W])
        ones_row = sb("ones_row", [1, P])
        ones_col = sb("ones_col", [P, 1])
        ident = sb("ident", [P, P])
        w1s = sb("w1s", [MUL0, MUL0])
        w2s = sb("w2s", [MUL0, MUL1])
        w3s = sb("w3s", [MUL1, MUL0])
        w4s = sb("w4s", [MUL1, MUL1])
        w5s = sb("w5s", [MUL1, MUL1])
        ws_s = sb("ws_s", [MUL0, MUL0])
        wv_s = sb("wv_s", [MUL1, MUL1])
        z = sb("z", [MUL0, 4, 4, D])
        L1 = sb("L1", [F1, 4, D])
        L2 = sb("L2", [P, D])

        pA1 = [ps(f"pA1_{k}", [P, 512]) for k in range(2)]
        pA2 = [ps(f"pA2_{k}", [P, 512]) for k in range(2)]
        pB1 = [ps(f"pB1_{k}", [P, 512]) for k in range(2)]
        pB2 = [ps(f"pB2_{k}", [P, 512]) for k in range(2)]
        banks = pA1 + pA2 + pB1 + pB2

        x_loaded = [sem(f"x_loaded{c}") for c in range(CHUNKS)]
        edges_loaded = sem("edges_loaded")
        weights_loaded = sem("weights_loaded")
        const_made = sem("const_made")
        eps_made = sem("eps_made")
        chain = sem("chain")
        var_ready = sem("var_ready")
        std_ready = sem("std_ready")
        norm_ready = sem("norm_ready")
        h_ready = sem("h_ready")
        xh_ready = sem("xh_ready")
        h_stored = [sem(f"h_stored{c}") for c in range(CHUNKS)]
        base_ready = sem("base_ready")
        base_spread = sem("base_spread")
        z_ready = sem("z_ready")
        L_product = sem("L_product")
        L_ready = sem("L_ready")
        idx_loaded = [sem(f"idx_loaded{k}") for k in range(2)]
        gathered = [sem(f"gathered{k}") for k in range(RING)]
        slot_seen_free = sem("slot_seen_free")
        onehot_made = sem("onehot_made")
        scat_ready = sem("scat_ready")
        agg_done = sem("agg_done")
        agg_copied = sem("agg_copied")
        mapped = sem("mapped")
        added = sem("added")
        outside_ready = sem("outside_ready")
        outside_counted = sem("outside_counted")
        counts_ready = sem("counts_ready")
        sums_ready = sem("sums_ready")
        left_dst = sem("left_dst")
        left_idx = sem("left_idx")
        left_rows = sem("left_rows")
        left_seen = sem("left_seen")
        left_group_done = sem("left_group_done")
        left_onehot = sem("left_onehot")
        left_scat = sem("left_scat")
        left_agg = sem("left_agg")
        left_copied = sem("left_copied")
        left_mapped = sem("left_mapped")
        left_added = sem("left_added")
        turned = sem("turned")
        finished = sem("finished")
        out_stored = sem("out_stored")

        block = ctx.enter_context(nc.Block())

        def edges_left(eng):
            eng.wait_ge(counts_ready, 2)
            return eng.value_load(n_out_all[0:1, 0:1], min_val=0, max_val=P * GROUPS)

        def group_left(eng, g):
            return eng.value_load(n_out[0:1, bass.ds(g, 1)], min_val=0, max_val=P)

        @block.sync
        def _(sp):
            for c in range(CHUNKS):
                cols = slice(c * CH * D, (c + 1) * CH * D)
                sp.dma_start(xh[:, c * CH:(c + 1) * CH, :].rearrange("p j d -> p (j d)"),
                             x_v[:, cols]).then_inc(x_loaded[c], 16)
            sp.dma_start(dst_i[:, :], dst).then_inc(edges_loaded, 16)
            sp.dma_start(sh_sb[:, :, :].rearrange("p t k -> p (t k)"), sh).then_inc(edges_loaded, 16)
            for t, w in ((w1s, w1t), (w2s, w2t), (w3s, w3t), (w4s, w4t), (w5s, w5t), (ws_s, ws), (wv_s, wv)):
                sp.dma_start(t[:, :], w).then_inc(weights_loaded, 16)
            for c in range(CHUNKS):
                sp.wait_ge(h_ready, CH * (c + 1))
                sp.dma_start(table_v[:, c * CH * D:(c + 1) * CH * D],
                             h[:, c % H_BUFS, :, :].rearrange("p j d -> p (j d)")).then_inc(h_stored[c], 16)
            with sp.Fori(0, TURNS) as i:
                for k in range(2):
                    sp.wait_ge(agg_done, i * RING + (k + 1) * HALF)
                    sp.dma_start(idx[k][:, :], src[:, bass.ds(i * (RING * TPG) + k * HALF * TPG, HALF * TPG)]
                                 ).then_inc(idx_loaded[k], 16)
            sp.wait_ge(agg_done, TURNS * RING + HALF)
            sp.dma_start(idx[0][:, 0:TAIL * TPG], src[:, TURNS * RING * TPG:TILES]).then_inc(idx_loaded[0], 16)
            with sp.If(edges_left(sp) > 0):
                sp.wait_ge(agg_done, GROUPS + RING)
                with sp.Fori(0, GROUPS) as g:
                    sp.wait_ge(left_group_done, g + 1)
                    sp.dma_start(idx[0][:, 0:TPG], src[:, bass.ds(g * TPG, TPG)]).then_inc(left_idx, 16)
            for n, j in enumerate(range(0, PER, BLK)):
                e = min(j + BLK, PER)
                sp.wait_ge(finished, n + 1)
                sp.dma_start(out_v[:, j * D:e * D], xh[:, j:e, :].rearrange("p j d -> p (j d)")
                             ).then_inc(out_stored, 16)
            sp.wait_ge(out_stored, 16 * -(-PER // BLK))

        @block.gpsimd
        def _(pool):
            pool.iota(iota_i[:, :], [[1, W]], base=0, channel_multiplier=0).then_inc(const_made, 1)
            pool.memset(ident[:, :], 0.0).then_inc(const_made, 1)
            pool.wait_ge(const_made, 2)
            pool.affine_select(out=ident[:, :], in_=ident[:, :], compare_op=ALU.not_equal, fill=1.0, base=0,
                               pattern=[[-1, P]], channel_multiplier=1).then_inc(const_made, 1)
            for c in range(CHUNKS):
                pool.wait_ge(h_stored[c], 16)

            def gather(slot, k, col):
                pool.indirect_dma_start(
                    out=rows[:, slot, k, :], out_offset=None, in_=table,
                    in_offset=bass.IndirectOffsetOnAxis(ap=idx[slot // HALF][:, col:col + 1], axis=0)
                ).then_inc(gathered[slot], 16)

            with pool.Fori(0, TURNS) as i:
                for u in range(RING):
                    if u % HALF == 0:
                        pool.wait_ge(idx_loaded[u // HALF], i * 16 + 16)
                    pool.wait_ge(agg_done, i * RING + u + 1)
                    pool.sem_inc(slot_seen_free, 1)
                    for k in range(TPG):
                        gather(u, k, (u % HALF) * TPG + k)
            pool.wait_ge(idx_loaded[0], 16 * (TURNS + 1))
            for u in range(TAIL):
                pool.wait_ge(agg_done, TURNS * RING + u + 1)
                for k in range(TPG):
                    gather(u, k, u * TPG + k)
            with pool.If(edges_left(pool) > 0):
                pool.wait_ge(agg_done, GROUPS + RING)
                with pool.Fori(0, GROUPS) as g:
                    pool.wait_ge(left_idx, g * 16 + 16)
                    pool.sem_inc(left_seen, 1)
                    for k in range(TPG):
                        pool.indirect_dma_start(
                            out=rows[:, 0, k, :], out_offset=None, in_=table,
                            in_offset=bass.IndirectOffsetOnAxis(ap=idx[0][:, k:k + 1], axis=0)
                        ).then_inc(left_rows, 16)

        @block.scalar
        def _(act):
            act.wait_ge(eps_made, 1)

            def take_root(c):
                js = slice(c * CH, (c + 1) * CH)
                act.wait_ge(var_ready, c + 1)
                nc.scalar.activation(std[:, js], mv[:, js, 1], ACT.Sqrt, bias=eps_t[0:NP, 0:1]).then_inc(std_ready, 1)

            take_root(0)
            for c in range(CHUNKS):
                if c + 1 < CHUNKS:
                    take_root(c + 1)
                act.wait_ge(norm_ready, c + 1)
                if c >= H_BUFS:
                    act.wait_ge(h_stored[c - H_BUFS], 16)
                    act.wait_ge(xh_ready, c - H_BUFS + 1)
                for j in range(c * CH, (c + 1) * CH):
                    nc.scalar.activation(h[:, c % H_BUFS, j - c * CH, :], xh[:, j, :], ACT.Relu,
                                         bias=shift[:, j:j + 1], scale=rstd[:, j:j + 1]).then_inc(h_ready, 1)
            act.wait_ge(L_product, 1)
            for k in range(4):
                nc.scalar.copy(L1[:, k, :], banks[k][:, 0:D]).then_inc(L_ready, 1)
            nc.scalar.copy(L2[:, :], banks[4][:, 0:D]).then_inc(L_ready, 1)

            def copy_sums(b, done, used):
                act.wait_ge(agg_done, done)
                act.wait_ge(mapped, used)
                act.sem_inc(slot_seen_free, 1)
                nc.scalar.copy(agg1[:, b, :, :].rearrange("p k w -> p (k w)"), pA1[b][:, 0:4 * W]
                               ).then_inc(agg_copied, 1)
                nc.scalar.copy(agg2[:, b, :], pA2[b][:, 0:W]).then_inc(agg_copied, 1)

            with act.Fori(0, TURNS) as i:
                for u in range(RING):
                    copy_sums(u % 2, i * RING + u + 1 + RING, i * RING + u + 1)
            for g in range(TURNS * RING, GROUPS):
                copy_sums(g % 2, g + 1 + RING, g + 1)
            with act.If(edges_left(act) > 0):
                act.wait_ge(mapped, GROUPS + 2)
                with act.Fori(0, GROUPS) as g:
                    with act.If(group_left(act, g) > 0):
                        with act.Fori(0, WINDOWS) as _j:
                            act.wait_ge(left_agg, 1)
                            act.sem_inc(left_agg, -1)
                            nc.scalar.copy(agg1[:, 0, :, :].rearrange("p k w -> p (k w)"), pA1[0][:, 0:4 * W]
                                           ).then_inc(left_copied, 1)
                            nc.scalar.copy(agg2[:, 0, :], pA2[0][:, 0:W]).then_inc(left_copied, 1)

        @block.vector
        def _(dve):
            steps = [0]

            def done(ins):
                steps[0] += 1
                ins.then_inc(chain, 1)
                return steps[0]

            dve.memset(eps_t[:, :], EPS).then_inc(eps_made, 1)
            dve.memset(ones_row[:, :], 1.0).then_inc(base_ready, 1)
            dve.memset(ones_col[:, :], 1.0).then_inc(outside_ready, 1)
            done(dve.memset(acc1[:, :], 0.0))
            done(dve.memset(acc2[:, :], 0.0))
            z_clear = done(dve.memset(z[:, :, :, :], 0.0))

            def layer_norm(c):
                js = slice(c * CH, (c + 1) * CH)
                dve.wait_ge(x_loaded[c], 16)
                for j in range(c * CH, (c + 1) * CH):
                    n = done(dve.bn_stats(stats[:, j, :], xh[:, j, :]))
                dve.wait_ge(chain, n)
                for j in range(c * CH, (c + 1) * CH):
                    ins = dve.bn_aggr(mv[:, j, :], stats[:, j, :])
                    n = done(ins)
                dve.wait_ge(chain, n)
                dve.sem_inc(var_ready, 1)
                dve.wait_ge(std_ready, c + 1)
                dve.wait_ge(chain, done(dve.reciprocal(rstd[:, js], std[:, js])))
                dve.scalar_tensor_tensor(out=shift[:, js], in0=mv[:, js, 0], scalar=-1.0, in1=rstd[:, js],
                                         op0=ALU.mult, op1=ALU.mult).then_inc(norm_ready, 1)

            def add_h(c):
                js = slice(c * CH, (c + 1) * CH)
                dve.wait_ge(h_ready, CH * (c + 1))
                dve.tensor_tensor(xh[:, js, :], xh[:, js, :], h[:, c % H_BUFS, :, :], ALU.add).then_inc(xh_ready, 1)

            for c in range(CHUNKS):
                if c >= H_BUFS:
                    add_h(c - H_BUFS)
                layer_norm(c)
            for c in range(CHUNKS - H_BUFS, CHUNKS):
                add_h(c)
            dve.wait_ge(edges_loaded, 32)
            dve.tensor_copy(base_f[:, :], dst_i[0:1, 0:TILES:TPG]).then_inc(base_ready, 1)
            done(dve.tensor_copy(base_i[:, :], dst_i[0:1, 0:TILES:TPG]))
            done(dve.tensor_copy(rel[:, :], dst_i[:, :]))
            dve.wait_ge(const_made, 3)
            n = done(dve.tensor_copy(iota_w[:, :], iota_i[:, :]))
            dve.wait_ge(chain, n)
            dve.wait_ge(base_spread, 1)
            rel_v = rel[:, :].rearrange("p (g t) -> p g t", t=TPG)
            n = done(dve.tensor_tensor(rel_v, rel_v, pA1[0][:, 0:GROUPS].unsqueeze(2).to_broadcast([P, GROUPS, TPG]),
                                       ALU.subtract))
            dve.wait_ge(chain, n)
            dve.sem_inc(base_spread, 1)
            n = done(dve.tensor_scalar(outside[:, :], rel[:, :], 0.0, None, ALU.is_lt))
            dve.wait_ge(chain, n)
            n = done(dve.scalar_tensor_tensor(out=outside[:, :], in0=rel[:, :], scalar=float(W), in1=outside[:, :],
                                              op0=ALU.is_ge, op1=ALU.max))
            dve.wait_ge(chain, n)
            dve.tensor_reduce(group_out[:, :], outside[:, :].rearrange("p (g t) -> p g t", t=TPG), AX_X, ALU.max
                              ).then_inc(outside_ready, 1)
            dve.wait_ge(outside_counted, 1)
            n = done(dve.tensor_reduce(n_out_f[:, :], pB2[1][0:1, 0:GROUPS], AX_X, ALU.add))
            dve.tensor_copy(n_out[:, :], pB2[1][0:1, 0:GROUPS]).then_inc(counts_ready, 1)
            dve.wait_ge(chain, n)
            dve.tensor_copy(n_out_all[:, :], n_out_f[:, :]).then_inc(counts_ready, 1)

            dve.wait_ge(weights_loaded, 16 * 7)
            dve.wait_ge(chain, z_clear)

            def put(block_, k, cols, w, scale):
                dve.tensor_scalar(z[0:w.shape[0], block_, k, cols], w[:, :], scale, None, ALU.mult
                                  ).then_inc(z_ready, 1)

            def vec(a):
                return slice(MUL0 + a, D, 3)

            n_put = 0
            put(0, 0, slice(0, MUL0), w1s, C0 * LIN_S)
            for a in range(3):
                put(0, 1 + a, vec(a), w2s, C0 * INV3 * LIN_S)
                put(1 + a, 1 + a, slice(0, MUL0), w3s, C1 * INV3 * LIN_V)
                put(1 + a, 0, vec(a), w4s, C1 * INV3 * LIN_V)
                for b in range(3):
                    if a != b:
                        sign = 1.0 if (b - a) % 3 == 1 else -1.0
                        put(1 + 3 - a - b, 1 + b, vec(a), w5s, sign * C1 * INV6 * LIN_V)

            def make_scatter(g, s, o, used):
                dve.tensor_tensor(onehot[:, o, :, :], iota_w[:, :].unsqueeze(1).to_broadcast([P, TPG, W]),
                                  rel[:, bass.ds(g * TPG, TPG)].unsqueeze(2).to_broadcast([P, TPG, W]),
                                  ALU.is_equal).then_inc(onehot_made, 1)
                dve.wait_ge(onehot_made, g + 1)
                dve.wait_ge(agg_done, used)
                dve.tensor_tensor(scat[:, s, :, :, :], onehot[:, o, :, :].unsqueeze(2).to_broadcast([P, TPG, 4, W]),
                                  sh_sb[:, bass.ds(g * TPG, TPG), :].unsqueeze(3).to_broadcast([P, TPG, 4, W]),
                                  ALU.mult).then_inc(scat_ready, 1)

            def add_window(g, b):
                base = dve.value_load(base_i[0:1, bass.ds(g, 1)], min_val=0, max_val=NODES - 1)
                dve.wait_ge(mapped, g + 3)
                dve.wait_ge(added, g * 2 + 4)
                dve.tensor_tensor(acc1[:, bass.ds(base, W)], acc1[:, bass.ds(base, W)], pB1[b][:, 0:W], ALU.add
                                  ).then_inc(added, 1)
                dve.tensor_tensor(acc2[:, bass.ds(base, W)], acc2[:, bass.ds(base, W)], pB2[b][0:F2, 0:W], ALU.add
                                  ).then_inc(added, 1)

            dve.sem_inc(added, 4)
            for g in range(LEAD):
                make_scatter(g, g, g % 2, RING)
            with dve.Fori(0, TURNS) as i:
                for u in range(RING):
                    make_scatter(i * RING + u + LEAD, (u + LEAD) % 4, u % 2, i * RING + u + LEAD + RING - 3)
                    add_window(i * RING + u, u % 2)
            for g in range(TURNS * RING, GROUPS):
                if g + LEAD < GROUPS:
                    make_scatter(g + LEAD, (g + LEAD) % 4, g % 2, g + LEAD + RING - 3)
                add_window(g, g % 2)

            dve.wait_ge(added, 2 * GROUPS + 4)
            with dve.If(edges_left(dve) > 0):
                dve.tensor_copy(rel[:, :], dst_i[:, :]).then_inc(left_dst, 1)
                dve.wait_ge(left_dst, 1)
                dve.scalar_tensor_tensor(out=rel[:, :], in0=rel[:, :], scalar=1.0, in1=outside[:, :],
                                         op0=ALU.add, op1=ALU.mult).then_inc(left_dst, 1)
                dve.wait_ge(left_dst, 2)
                dve.tensor_scalar(rel[:, :], rel[:, :], -1.0, None, ALU.add).then_inc(left_dst, 1)
                dve.wait_ge(left_dst, 3)
                with dve.Fori(0, GROUPS) as g:
                    with dve.If(group_left(dve, g) > 0):
                        with dve.Fori(0, WINDOWS) as j:
                            dve.tensor_tensor(onehot[:, 0, :, :],
                                              iota_w[:, :].unsqueeze(1).to_broadcast([P, TPG, W]),
                                              rel[:, bass.ds(g * TPG, TPG)].unsqueeze(2).to_broadcast([P, TPG, W]),
                                              ALU.is_equal).then_inc(left_onehot, 1)
                            dve.wait_ge(left_onehot, 1)
                            dve.sem_inc(left_onehot, -1)
                            dve.tensor_tensor(
                                scat[:, 0, :, :, :], onehot[:, 0, :, :].unsqueeze(2).to_broadcast([P, TPG, 4, W]),
                                sh_sb[:, bass.ds(g * TPG, TPG), :].unsqueeze(3).to_broadcast([P, TPG, 4, W]),
                                ALU.mult).then_inc(left_scat, 1)
                            dve.tensor_scalar(rel[:, bass.ds(g * TPG, TPG)], rel[:, bass.ds(g * TPG, TPG)],
                                              -float(W), None, ALU.add).then_inc(left_added, 1)
                            dve.wait_ge(left_mapped, 1)
                            dve.sem_inc(left_mapped, -1)
                            here = bass.ds(j * W, W)
                            dve.tensor_tensor(acc1[:, here], acc1[:, here], pB1[0][:, 0:W], ALU.add
                                              ).then_inc(left_added, 1)
                            dve.tensor_tensor(acc2[:, here], acc2[:, here], pB2[0][0:F2, 0:W], ALU.add
                                              ).then_inc(left_added, 1)
                            dve.wait_ge(left_added, 3)
                            dve.sem_inc(left_added, -3)
            dve.sem_inc(sums_ready, 1)

            for n, j in enumerate(range(0, PER, BLK)):
                e = min(j + BLK, PER)
                dve.wait_ge(turned, n + 1)
                dve.scalar_tensor_tensor(out=xh[:, j:e, :], in0=banks[n % 8][0:NP, 0:(e - j) * D].rearrange(
                    "p (j d) -> p j d", d=D), scalar=0.0, in1=xh[:, j:e, :], op0=ALU.max, op1=ALU.add
                ).then_inc(finished, 1)

        @block.tensor
        def _(pe):
            pe.sem_inc(agg_done, RING)
            pe.sem_inc(mapped, 2)
            pe.sem_inc(agg_copied, 2)
            pe.wait_ge(base_ready, 2)
            nc.tensor.matmul(pA1[0][:, 0:GROUPS], ones_row[:, :], base_f[:, :], start=True, stop=True
                             ).then_inc(base_spread, 1)
            pe.wait_ge(base_spread, 2)
            pe.wait_ge(outside_ready, 2)
            nc.tensor.matmul(pB2[1][0:1, 0:GROUPS], ones_col[:, :], group_out[:, :], start=True, stop=True
                             ).then_inc(outside_counted, 1)
            pe.wait_ge(z_ready, 16)
            for blk in range(4):
                kk, w = (MUL0, ws_s) if blk == 0 else (MUL1, wv_s)
                cols = slice(0, MUL0) if blk == 0 else slice(MUL0 + blk - 1, D, 3)
                for k in range(4):
                    nc.tensor.matmul(banks[k][:, cols], z[0:kk, blk, k, 0:F1], w[:, :], start=True, stop=True)
                    last = nc.tensor.matmul(banks[4][F2 * k:F2 * k + F2, cols], z[0:kk, blk, k, F1:D], w[:, :],
                                            start=True, stop=True, tile_position=(0, F2 * k))
            last.then_inc(L_product, 1)
            pe.wait_ge(L_ready, 5)

            def sum_window(slot, s, b):
                for t in range(TPG):
                    nc.tensor.matmul(pA1[b][:, 0:4 * W], rows[:, slot, t, 0:F1],
                                     scat[:, s, t, :, :].rearrange("p k w -> p (k w)"),
                                     start=(t == 0), stop=(t == TPG - 1))
                for t in range(TPG):
                    for k in range(4):
                        last = nc.tensor.matmul(pA2[b][32 * k:32 * k + F2, 0:W], rows[:, slot, t, F1:D],
                                                scat[:, s, t, k, :], start=(t == 0), stop=(t == TPG - 1),
                                                tile_position=(0, 32 * k))
                return last

            def map_sums(b):
                for o, cols in ((pB1[b][:, 0:W], slice(0, F1)), (pB2[b][0:F2, 0:W], slice(F1, D))):
                    for k in range(4):
                        nc.tensor.matmul(o, L1[:, k, cols], agg1[:, b, k, :], start=(k == 0), stop=False)
                    last = nc.tensor.matmul(o, L2[:, cols], agg2[:, b, :], start=False, stop=True)
                return last

            def aggregate(slot, s, b, landed, scattered, copied):
                pe.wait_ge(gathered[slot], landed)
                pe.wait_ge(scat_ready, scattered)
                pe.wait_ge(agg_copied, copied)
                pe.sem_inc(slot_seen_free, 1)
                sum_window(slot, s, b).then_inc(agg_done, 1)

            def map_window(b, copied, free):
                pe.wait_ge(agg_copied, copied)
                pe.wait_ge(added, free)
                pe.sem_inc(slot_seen_free, 1)
                map_sums(b).then_inc(mapped, 1)

            aggregate(0, 0, 0, 16 * TPG, 1, 2)
            with pe.Fori(0, TURNS) as i:
                for u in range(RING):
                    v = u + 1
                    aggregate(v % RING, v % 4, v % 2, (i + v // RING) * (16 * TPG) + 16 * TPG, i * RING + v + 1,
                              (i * RING + v) * 2)
                    map_window(u % 2, (i * RING + u) * 2 + 4, (i * RING + u) * 2 + 2)
            for g in range(TURNS * RING, GROUPS):
                if g + 1 < GROUPS:
                    v = g + 1
                    aggregate(v % RING, v % 4, v % 2, (v // RING + 1) * 16 * TPG, v + 1, 2 * v)
                map_window(g % 2, 2 * g + 4, 2 * g + 2)

            with pe.If(edges_left(pe) > 0):
                pe.wait_ge(added, 2 * GROUPS + 4)
                pe.sem_inc(left_group_done, 1)
                with pe.Fori(0, GROUPS) as g:
                    pe.wait_ge(left_rows, g * (16 * TPG) + 16 * TPG)
                    with pe.If(group_left(pe, g) > 0):
                        with pe.Fori(0, WINDOWS) as _j:
                            pe.wait_ge(left_scat, 1)
                            pe.sem_inc(left_scat, -1)
                            sum_window(0, 0, 0).then_inc(left_agg, 1)
                            pe.wait_ge(left_copied, 2)
                            pe.sem_inc(left_copied, -2)
                            map_sums(0).then_inc(left_mapped, 1)
                    pe.sem_inc(left_group_done, 1)

            pe.wait_ge(sums_ready, 1)
            pe.wait_ge(const_made, 3)
            for n, j in enumerate(range(0, PER, BLK)):
                if n >= 8:
                    pe.wait_ge(finished, n - 7)
                for q in range(j, min(j + BLK, PER)):
                    o = banks[n % 8][0:NP, (q - j) * D:(q - j + 1) * D]
                    nc.tensor.transpose(o[:, 0:F1], acc1[:, q:q + (NP - 1) * PER + 1:PER], ident[:, :])
                    last = nc.tensor.transpose(o[:, F1:D], acc2[:, q:q + (NP - 1) * PER + 1:PER], ident[0:F2, 0:F2])
                last.then_inc(turned, 1)


_INS = ["x", "src", "dst", "sh", "w1t", "w2t", "w3t", "w4t", "w5t", "ws", "wv"]


def kernel(x, src, dst, edge_attr_4, L0_gnn_W1, L0_gnn_W2, L0_gnn_W3, L0_gnn_W4, L0_gnn_W5, L0_gnn_Ws, L0_gnn_Wv):
    import numpy as _np
    import concourse.bacc as _bacc
    from concourse import mybir as _mybir
    from concourse.bass_utils import run_bass_kernel_spmd as _run

    pad = TILES * P - EDGES
    src_t = _np.pad(_np.asarray(src), (0, pad), mode="edge").reshape(TILES, P).T
    dst_t = _np.pad(_np.asarray(dst), (0, pad), mode="edge").reshape(TILES, P).T
    sh_t = _np.pad(_np.asarray(edge_attr_4), ((0, pad), (0, 0))).reshape(TILES, P, 4).transpose(1, 0, 2).reshape(
        P, TILES * 4)
    values = [x, src_t, dst_t, sh_t, _np.asarray(L0_gnn_W1).T, _np.asarray(L0_gnn_W2).T, _np.asarray(L0_gnn_W3).T,
              _np.asarray(L0_gnn_W4).T, _np.asarray(L0_gnn_W5).T, L0_gnn_Ws, L0_gnn_Wv]

    nc = _bacc.Bacc("TRN2", target_bir_lowering=False, num_devices=1)
    arrays, args = {}, []
    for name, value in zip(_INS, values):
        a = _np.ascontiguousarray(value)
        arrays[f"in_{name}_dram"] = a
        args.append(nc.dram_tensor(f"in_{name}_dram", a.shape, _mybir.dt.from_np(a.dtype), kind="ExternalInput").ap())
    args.append(nc.dram_tensor("table_dram", (NODES, D), F32, kind="Internal").ap())
    args.append(nc.dram_tensor("out_0_dram", (NODES, D), F32, kind="ExternalOutput").ap())
    gnn_kernel(nc, *args)
    r = _run(nc, [arrays], core_ids=[0])
    return r.results[0]["out_0_dram"]
```

```python
from contextlib import ExitStack

import concourse.bass as bass
from concourse import mybir

F32 = mybir.dt.float32
I32 = mybir.dt.int32
ALU = mybir.AluOpType
ACT = mybir.ActivationFunctionType
AX_X = mybir.AxisListType.X

NODES = 6250
MUL0, MUL1 = 64, 32
D = MUL0 + 3 * MUL1
EDGES = 206250
EPS = 1e-5

C0 = (MUL0 + MUL1) ** -0.5
C1 = (3.0 / (MUL0 + 2 * MUL1)) ** 0.5
INV3 = 3.0 ** -0.5
INV6 = 6.0 ** -0.5
LIN_S = MUL0 ** -0.5
LIN_V = MUL1 ** -0.5

P = 128
TPG = 4
W = 24
GROUPS = -(-EDGES // (P * TPG))
TILES = GROUPS * TPG
RING = 8
HALF = RING // 2
TURNS = (GROUPS - 1) // RING
TAIL = GROUPS - TURNS * RING
LAST_HALF = 2 * TURNS
CHECK_TURN = 4
PAIRS = RING // 2
SH_FIRST = 3 * RING * TPG
LEAD = 2
assert LEAD <= TAIL <= HALF

NP = 125
PER = NODES // NP
CHUNKS = 5
CH = PER // CHUNKS
H_BUFS = CHUNKS - 1
BLK = 3
WINDOWS = -(-NODES // W)
COLS = WINDOWS * W + W
F1, F2 = P, D - P


def gnn_kernel(nc: bass.Bass, x, src, dst, sh, w1t, w2t, w3t, w4t, w5t, ws, wv, table, out):
    x_v = x.rearrange("(p j) d -> p (j d)", p=NP)
    table_v = table.rearrange("(p j) d -> p (j d)", p=NP)
    out_v = out.rearrange("(p j) d -> p (j d)", p=NP)

    with ExitStack() as ctx:
        def sb(name, shape, dt=F32):
            return ctx.enter_context(nc.sbuf_tensor(name, shape, dt))

        def ps(name, shape):
            return ctx.enter_context(nc.psum_tensor(name, shape, F32))

        def sem(name):
            return ctx.enter_context(nc.semaphore(name))

        xh = sb("xh", [NP, PER, D])
        h = sb("h", [NP, H_BUFS, CH, D])
        stats = sb("stats", [NP, PER, 6])
        mv = sb("mv", [NP, PER, 2])
        std = sb("std", [NP, PER])
        rstd = sb("rstd", [NP, PER])
        shift = sb("shift", [NP, PER])
        eps_t = sb("eps_t", [P, 1])
        acc1 = sb("acc1", [F1, COLS])
        acc2 = sb("acc2", [F2, COLS])
        dst_i = sb("dst_i", [P, TILES], I32)
        rel = sb("rel", [P, TILES])
        sh_sb = sb("sh_sb", [P, TILES, 4])
        idx = [sb(f"idx{k}", [P, HALF * TPG], I32) for k in range(2)]
        idx_first = [sb(f"idx_first{k}", [P, HALF * TPG], I32) for k in range(2)]
        base_f = sb("base_f", [1, GROUPS])
        base_i = sb("base_i", [1, GROUPS], I32)
        outside = sb("outside", [P, TILES])
        group_out = sb("group_out", [P, GROUPS])
        n_out = sb("n_out", [1, GROUPS], I32)
        n_out_f = sb("n_out_f", [1, 1])
        n_out_all = sb("n_out_all", [1, 1], I32)
        rows = sb("rows", [P, RING, TPG, D])
        row_stats = sb("row_stats", [P, PAIRS, 2 * TPG, 6])
        row_mv = sb("row_mv", [P, PAIRS, 2 * TPG, 2])
        row_std = sb("row_std", [P, PAIRS, 2 * TPG])
        row_rstd = sb("row_rstd", [P, PAIRS, 2 * TPG])
        row_shift = sb("row_shift", [P, PAIRS, 2 * TPG])
        onehot = sb("onehot", [P, 2, TPG, W])
        scat = sb("scat", [P, 4, TPG, 4, W])
        agg1 = sb("agg1", [F1, 2, 4, HALF * W])
        agg2 = sb("agg2", [P, 2, HALF * W])
        iota_i = sb("iota_i", [P, W], I32)
        iota_w = sb("iota_w", [P, W])
        ones_row = sb("ones_row", [1, P])
        ones_col = sb("ones_col", [P, 1])
        ident = sb("ident", [P, P])
        w1s = sb("w1s", [MUL0, MUL0])
        w2s = sb("w2s", [MUL0, MUL1])
        w3s = sb("w3s", [MUL1, MUL0])
        w4s = sb("w4s", [MUL1, MUL1])
        w5s = sb("w5s", [MUL1, MUL1])
        ws_s = sb("ws_s", [MUL0, MUL0])
        wv_s = sb("wv_s", [MUL1, MUL1])
        z = sb("z", [MUL0, 4, 4, D])
        L1 = sb("L1", [F1, 4, D])
        L2 = sb("L2", [P, D])

        pA1 = [ps(f"pA1_{k}", [P, 512]) for k in range(2)]
        pA2 = [ps(f"pA2_{k}", [P, 512]) for k in range(2)]
        pB1 = [ps(f"pB1_{k}", [P, 512]) for k in range(2)]
        pB2 = [ps(f"pB2_{k}", [P, 512]) for k in range(2)]
        banks = pA1 + pA2 + pB1 + pB2

        x_loaded = [sem(f"x_loaded{c}") for c in range(CHUNKS)]
        dst_loaded = sem("dst_loaded")
        sh_loaded = [sem(f"sh_loaded{k}") for k in range(2)]
        weights_loaded = sem("weights_loaded")
        const_made = sem("const_made")
        eps_made = sem("eps_made")
        chain = sem("chain")
        var_ready = sem("var_ready")
        std_ready = sem("std_ready")
        norm_ready = sem("norm_ready")
        h_ready = sem("h_ready")
        xh_ready = sem("xh_ready")
        h_stored = [sem(f"h_stored{c}") for c in range(CHUNKS)]
        base_ready = sem("base_ready")
        base_spread = sem("base_spread")
        z_ready = sem("z_ready")
        L_product = sem("L_product")
        L_ready = sem("L_ready")
        idx_first_loaded = [sem(f"idx_first_loaded{k}") for k in range(2)]
        idx_loaded = [sem(f"idx_loaded{k}") for k in range(2)]
        gathered = [sem(f"gathered{k}") for k in range(RING)]
        slot_seen_free = sem("slot_seen_free")
        onehot_made = sem("onehot_made")
        scat_ready = sem("scat_ready")
        agg_done = sem("agg_done")
        row_var_ready = sem("row_var_ready")
        row_std_ready = sem("row_std_ready")
        row_norm_ready = sem("row_norm_ready")
        rows_normed = sem("rows_normed")
        zeroed = sem("zeroed")
        acc2_zeroed = sem("acc2_zeroed")
        agg_copied = sem("agg_copied")
        mapped = sem("mapped")
        added = sem("added")
        outside_ready = sem("outside_ready")
        outside_counted = sem("outside_counted")
        counts_ready = sem("counts_ready")
        sums_ready = sem("sums_ready")
        left_dst = sem("left_dst")
        left_idx = sem("left_idx")
        left_rows = sem("left_rows")
        left_seen = sem("left_seen")
        left_group_done = sem("left_group_done")
        left_onehot = sem("left_onehot")
        left_scat = sem("left_scat")
        left_agg = sem("left_agg")
        left_copied = sem("left_copied")
        left_mapped = sem("left_mapped")
        left_added = sem("left_added")
        turned = sem("turned")
        finished = sem("finished")
        out_stored = sem("out_stored")

        block = ctx.enter_context(nc.Block())

        def half_view(bank):
            return bank[:, 0:4 * HALF * W].rearrange("p (k n) -> p k n", k=4)

        def edges_left(eng):
            eng.wait_ge(counts_ready, 2)
            return eng.value_load(n_out_all[0:1, 0:1], min_val=0, max_val=P * GROUPS)

        def group_left(eng, g):
            return eng.value_load(n_out[0:1, bass.ds(g, 1)], min_val=0, max_val=P)

        @block.sync
        def _(sp):
            for k in range(2):
                sp.dma_start(idx_first[k][:, :], src[:, k * HALF * TPG:(k + 1) * HALF * TPG]
                             ).then_inc(idx_first_loaded[k], 16)
            for c in range(CHUNKS):
                cols = slice(c * CH * D, (c + 1) * CH * D)
                sp.dma_start(xh[:, c * CH:(c + 1) * CH, :].rearrange("p j d -> p (j d)"),
                             x_v[:, cols]).then_inc(x_loaded[c], 16)
            for t, w in ((w1s, w1t), (w2s, w2t), (w3s, w3t), (w4s, w4t), (w5s, w5t), (ws_s, ws), (wv_s, wv)):
                sp.dma_start(t[:, :], w).then_inc(weights_loaded, 16)
            for k in range(2):
                at = (RING + k * HALF) * TPG
                sp.dma_start(idx[k][:, :], src[:, at:at + HALF * TPG]).then_inc(idx_loaded[k], 16)
            sp.dma_start(dst_i[:, :], dst).then_inc(dst_loaded, 16)
            sh_tiles = sh_sb[:, :, :].rearrange("p t k -> p (t k)")
            sp.dma_start(sh_tiles[:, 0:4 * SH_FIRST], sh[:, 0:4 * SH_FIRST]).then_inc(sh_loaded[0], 16)
            sp.wait_ge(zeroed, 1)
            sp.dma_start(acc2[:, :], acc1[0:F2, :]).then_inc(acc2_zeroed, 16)
            for c in range(CHUNKS):
                sp.wait_ge(h_ready, CH * (c + 1))
                sp.dma_start(table_v[:, c * CH * D:(c + 1) * CH * D],
                             h[:, c % H_BUFS, :, :].rearrange("p j d -> p (j d)")).then_inc(h_stored[c], 16)
            sp.dma_start(sh_tiles[:, 4 * SH_FIRST:], sh[:, 4 * SH_FIRST:]).then_inc(sh_loaded[1], 16)
            with sp.Fori(2, TURNS) as i:
                for k in range(2):
                    sp.wait_ge(agg_done, i * RING + (k + 1) * HALF)
                    sp.dma_start(idx[k][:, :], src[:, bass.ds(i * (RING * TPG) + k * HALF * TPG, HALF * TPG)]
                                 ).then_inc(idx_loaded[k], 16)
            sp.wait_ge(agg_done, TURNS * RING + HALF)
            sp.dma_start(idx[0][:, 0:TAIL * TPG], src[:, TURNS * RING * TPG:TILES]).then_inc(idx_loaded[0], 16)
            with sp.If(edges_left(sp) > 0):
                sp.wait_ge(agg_done, GROUPS + RING)
                with sp.Fori(0, GROUPS) as g:
                    sp.wait_ge(left_group_done, g + 1)
                    sp.dma_start(idx[0][:, 0:TPG], src[:, bass.ds(g * TPG, TPG)]).then_inc(left_idx, 16)
            for n, j in enumerate(range(0, PER, BLK)):
                e = min(j + BLK, PER)
                sp.wait_ge(finished, n + 1)
                sp.dma_start(out_v[:, j * D:e * D], xh[:, j:e, :].rearrange("p j d -> p (j d)")
                             ).then_inc(out_stored, 16)
            sp.wait_ge(out_stored, 16 * -(-PER // BLK))

        @block.gpsimd
        def _(pool):
            pool.iota(iota_i[:, :], [[1, W]], base=0, channel_multiplier=0).then_inc(const_made, 1)
            pool.memset(ident[:, :], 0.0).then_inc(const_made, 1)
            pool.wait_ge(const_made, 2)
            pool.affine_select(out=ident[:, :], in_=ident[:, :], compare_op=ALU.not_equal, fill=1.0, base=0,
                               pattern=[[-1, P]], channel_multiplier=1).then_inc(const_made, 1)

            def gather(slot, k, col, of=table, by=idx):
                pool.indirect_dma_start(
                    out=rows[:, slot, k, :], out_offset=None, in_=of,
                    in_offset=bass.IndirectOffsetOnAxis(ap=by[slot // HALF][:, col:col + 1], axis=0)
                ).then_inc(gathered[slot], 16)

            for u in range(RING):
                if u % HALF == 0:
                    pool.wait_ge(idx_first_loaded[u // HALF], 16)
                for k in range(TPG):
                    gather(u, k, (u % HALF) * TPG + k, x, idx_first)
            for c in range(CHUNKS):
                pool.wait_ge(h_stored[c], 16)
            with pool.Fori(1, TURNS) as i:
                for u in range(RING):
                    if u % HALF == 0:
                        pool.wait_ge(idx_loaded[u // HALF], i * 16)
                    pool.wait_ge(agg_done, i * RING + u + 1)
                    pool.sem_inc(slot_seen_free, 1)
                    for k in range(TPG):
                        gather(u, k, (u % HALF) * TPG + k)
            pool.wait_ge(idx_loaded[0], 16 * TURNS)
            for u in range(TAIL):
                pool.wait_ge(agg_done, TURNS * RING + u + 1)
                for k in range(TPG):
                    gather(u, k, u * TPG + k)
            with pool.If(edges_left(pool) > 0):
                pool.wait_ge(agg_done, GROUPS + RING)
                with pool.Fori(0, GROUPS) as g:
                    pool.wait_ge(left_idx, g * 16 + 16)
                    pool.sem_inc(left_seen, 1)
                    for k in range(TPG):
                        pool.indirect_dma_start(
                            out=rows[:, 0, k, :], out_offset=None, in_=table,
                            in_offset=bass.IndirectOffsetOnAxis(ap=idx[0][:, k:k + 1], axis=0)
                        ).then_inc(left_rows, 16)

        @block.scalar
        def _(act):
            act.wait_ge(eps_made, 2)
            nc.scalar.activation(acc1[:, :], ones_col[:, 0:1].to_broadcast([P, COLS]), ACT.Copy, scale=0.0
                                 ).then_inc(zeroed, 1)

            def take_root(c):
                js = slice(c * CH, (c + 1) * CH)
                act.wait_ge(var_ready, c + 1)
                nc.scalar.activation(std[:, js], mv[:, js, 1], ACT.Sqrt, bias=eps_t[0:NP, 0:1]).then_inc(std_ready, 1)

            take_root(0)
            for c in range(CHUNKS):
                if c + 1 < CHUNKS:
                    take_root(c + 1)
                act.wait_ge(norm_ready, c + 1)
                if c >= H_BUFS:
                    act.wait_ge(h_stored[c - H_BUFS], 16)
                    act.wait_ge(xh_ready, c - H_BUFS + 1)
                for j in range(c * CH, (c + 1) * CH):
                    nc.scalar.activation(h[:, c % H_BUFS, j - c * CH, :], xh[:, j, :], ACT.Relu,
                                         bias=shift[:, j:j + 1], scale=rstd[:, j:j + 1]).then_inc(h_ready, 1)
            def copy_sums(b, done, used, groups=HALF):
                act.wait_ge(agg_done, done)
                act.wait_ge(mapped, used)
                act.sem_inc(slot_seen_free, 1)
                n = groups * W
                nc.scalar.copy(agg1[:, b, :, 0:n], half_view(pA1[b])[:, :, 0:n]).then_inc(agg_copied, 1)
                nc.scalar.copy(agg2[:, b, 0:n], pA2[b][:, 0:n]).then_inc(agg_copied, 1)

            def row_root(q):
                act.wait_ge(row_var_ready, q + 1)
                nc.scalar.activation(row_std[:, q, :], row_mv[:, q, :, 1], ACT.Sqrt, bias=eps_t[:, 0:1]
                                     ).then_inc(row_std_ready, 1)

            def norm_rows(q):
                act.wait_ge(row_norm_ready, q + 1)
                for n in range(2 * TPG):
                    r = rows[:, 2 * q + n // TPG, n % TPG, :]
                    nc.scalar.activation(r, r, ACT.Relu, bias=row_shift[:, q, n:n + 1],
                                         scale=row_rstd[:, q, n:n + 1]).then_inc(rows_normed, 1)

            act.wait_ge(L_product, 1)
            for k in range(4):
                nc.scalar.copy(L1[:, k, :], banks[k][:, 0:D]).then_inc(L_ready, 1)
            nc.scalar.copy(L2[:, :], banks[4][:, 0:D]).then_inc(L_ready, 1)

            row_root(0)
            for q in range(PAIRS + 1):
                if q + 1 < PAIRS:
                    row_root(q + 1)
                if q < PAIRS:
                    norm_rows(q)
                if q in (2, 4):
                    hf = q // 2 - 1
                    copy_sums(hf, (hf + 1) * HALF + RING, hf + 1)
            with act.Fori(1, TURNS) as i:
                for hf in range(2):
                    copy_sums(hf, i * RING + (hf + 1) * HALF + RING, i * 2 + hf + 1)
            copy_sums(0, GROUPS + RING, LAST_HALF + 1, TAIL)
            with act.If(edges_left(act) > 0):
                act.wait_ge(mapped, LAST_HALF + 1 + 2)
                with act.Fori(0, GROUPS) as g:
                    with act.If(group_left(act, g) > 0):
                        with act.Fori(0, WINDOWS) as _j:
                            act.wait_ge(left_agg, 1)
                            act.sem_inc(left_agg, -1)
                            nc.scalar.copy(agg1[:, 0, :, 0:W], half_view(pA1[0])[:, :, 0:W]
                                           ).then_inc(left_copied, 1)
                            nc.scalar.copy(agg2[:, 0, 0:W], pA2[0][:, 0:W]).then_inc(left_copied, 1)

        @block.vector
        def _(dve):
            steps = [0]

            def done(ins):
                steps[0] += 1
                ins.then_inc(chain, 1)
                return steps[0]

            dve.memset(eps_t[:, :], EPS).then_inc(eps_made, 1)
            dve.memset(ones_row[:, :], 1.0).then_inc(base_ready, 1)
            dve.memset(ones_col[:, :], 1.0).then_inc(eps_made, 1)
            dve.memset(z[:, :, :, :], 0.0).then_inc(eps_made, 1)

            def node_sums(c):
                dve.wait_ge(x_loaded[c], 16)
                for j in range(c * CH, (c + 1) * CH):
                    n = done(dve.bn_stats(stats[:, j, :], xh[:, j, :]))
                dve.wait_ge(chain, n)
                for j in range(c * CH, (c + 1) * CH):
                    ins = dve.bn_aggr(mv[:, j, :], stats[:, j, :])
                    n = done(ins)
                dve.wait_ge(chain, n)
                dve.sem_inc(var_ready, 1)

            def node_scale(c):
                js = slice(c * CH, (c + 1) * CH)
                dve.wait_ge(std_ready, c + 1)
                dve.wait_ge(chain, done(dve.reciprocal(rstd[:, js], std[:, js])))
                dve.scalar_tensor_tensor(out=shift[:, js], in0=mv[:, js, 0], scalar=-1.0, in1=rstd[:, js],
                                         op0=ALU.mult, op1=ALU.mult).then_inc(norm_ready, 1)

            def add_h(c):
                js = slice(c * CH, (c + 1) * CH)
                dve.wait_ge(h_ready, CH * (c + 1))
                dve.tensor_tensor(xh[:, js, :], xh[:, js, :], h[:, c % H_BUFS, :, :], ALU.add).then_inc(xh_ready, 1)

            def vec(a):
                return slice(MUL0 + a, D, 3)

            def put(block_, k, cols, w, scale):
                dve.tensor_scalar(z[0:w.shape[0], block_, k, cols], w[:, :], scale, None, ALU.mult
                                  ).then_inc(z_ready, 1)

            def put_weights():
                dve.wait_ge(weights_loaded, 16 * 7)
                dve.wait_ge(eps_made, 3)
                put(0, 0, slice(0, MUL0), w1s, C0 * LIN_S)
                for a in range(3):
                    put(0, 1 + a, vec(a), w2s, C0 * INV3 * LIN_S)
                    put(1 + a, 1 + a, slice(0, MUL0), w3s, C1 * INV3 * LIN_V)
                    put(1 + a, 0, vec(a), w4s, C1 * INV3 * LIN_V)
                    for b in range(3):
                        if a != b:
                            sign = 1.0 if (b - a) % 3 == 1 else -1.0
                            put(1 + 3 - a - b, 1 + b, vec(a), w5s, sign * C1 * INV6 * LIN_V)

            node_sums(0)
            for c in range(CHUNKS):
                if c + 1 < CHUNKS:
                    node_sums(c + 1)
                node_scale(c)
                if c == 2:
                    put_weights()
            for c in range(CHUNKS - H_BUFS):
                add_h(c)
            dve.wait_ge(dst_loaded, 16)
            dve.tensor_copy(base_f[:, :], dst_i[0:1, 0:TILES:TPG]).then_inc(base_ready, 1)
            done(dve.tensor_copy(base_i[:, :], dst_i[0:1, 0:TILES:TPG]))
            done(dve.tensor_copy(rel[:, :], dst_i[:, :]))
            dve.wait_ge(const_made, 3)
            n = done(dve.tensor_copy(iota_w[:, :], iota_i[:, :]))
            dve.wait_ge(chain, n)
            dve.wait_ge(base_spread, 1)
            rel_v = rel[:, :].rearrange("p (g t) -> p g t", t=TPG)
            n = done(dve.tensor_tensor(rel_v, rel_v, pB1[1][:, 0:GROUPS].unsqueeze(2).to_broadcast([P, GROUPS, TPG]),
                                       ALU.subtract))
            dve.wait_ge(chain, n)
            dve.sem_inc(base_spread, 1)
            def make_scatter(g, s, o, used):
                dve.tensor_tensor(onehot[:, o, :, :], iota_w[:, :].unsqueeze(1).to_broadcast([P, TPG, W]),
                                  rel[:, bass.ds(g * TPG, TPG)].unsqueeze(2).to_broadcast([P, TPG, W]),
                                  ALU.is_equal).then_inc(onehot_made, 1)
                dve.wait_ge(onehot_made, g + 1)
                dve.wait_ge(agg_done, used)
                dve.tensor_tensor(scat[:, s, :, :, :], onehot[:, o, :, :].unsqueeze(2).to_broadcast([P, TPG, 4, W]),
                                  sh_sb[:, bass.ds(g * TPG, TPG), :].unsqueeze(3).to_broadcast([P, TPG, 4, W]),
                                  ALU.mult).then_inc(scat_ready, 1)

            def first_node(g):
                return dve.value_load(base_i[0:1, bass.ds(g, 1)], min_val=0, max_val=NODES - 1)

            def add_window(g, m, b, mapped_halves, base=None):
                if base is None:
                    base = first_node(g)
                dve.wait_ge(mapped, mapped_halves)
                dve.wait_ge(added, g * 2 + 4 * HALF)
                dve.tensor_tensor(acc1[:, bass.ds(base, W)], acc1[:, bass.ds(base, W)],
                                  pB1[b][:, m * W:(m + 1) * W], ALU.add).then_inc(added, 1)
                dve.tensor_tensor(acc2[:, bass.ds(base, W)], acc2[:, bass.ds(base, W)],
                                  pB2[b][0:F2, m * W:(m + 1) * W], ALU.add).then_inc(added, 1)

            def row_sums(q):
                for g in (2 * q, 2 * q + 1):
                    dve.wait_ge(gathered[g], 16 * TPG)
                for m in range(2 * TPG):
                    n = done(dve.bn_stats(row_stats[:, q, m, :], rows[:, 2 * q + m // TPG, m % TPG, :]))
                dve.wait_ge(chain, n)
                for m in range(2 * TPG):
                    ins = dve.bn_aggr(row_mv[:, q, m, :], row_stats[:, q, m, :])
                    n = done(ins)
                dve.wait_ge(chain, n)
                dve.sem_inc(row_var_ready, 1)

            def row_scale(q):
                dve.wait_ge(row_std_ready, q + 1)
                dve.wait_ge(chain, done(dve.reciprocal(row_rstd[:, q, :], row_std[:, q, :])))
                dve.scalar_tensor_tensor(out=row_shift[:, q, :], in0=row_mv[:, q, :, 0], scalar=-1.0,
                                         in1=row_rstd[:, q, :], op0=ALU.mult, op1=ALU.mult
                                         ).then_inc(row_norm_ready, 1)

            def first_turn(g):
                make_scatter(g + LEAD, (g + LEAD) % 4, g % 2, g + LEAD + RING - 3)
                if g >= HALF:
                    add_window(g - HALF, g - HALF, 0, 3)

            dve.sem_inc(added, 4 * HALF)
            row_sums(0)
            row_sums(1)
            row_scale(0)
            dve.wait_ge(sh_loaded[0], 16)
            for g in range(LEAD):
                make_scatter(g, g, g % 2, RING)
            dve.wait_ge(zeroed, 1)
            dve.wait_ge(acc2_zeroed, 16)
            for q in range(1, PAIRS + 1):
                if q + 1 < PAIRS:
                    row_sums(q + 1)
                if q < PAIRS:
                    row_scale(q)
                for g in (2 * q - 2, 2 * q - 1):
                    first_turn(g)
                if q < CHUNKS:
                    add_h(q)
            dve.wait_ge(sh_loaded[1], 16)

            def turn(i):
                for u in range(RING):
                    make_scatter(i * RING + u + LEAD, (u + LEAD) % 4, u % 2, i * RING + u + LEAD + RING - 3)
                    add_window(i * RING + u - HALF, u % HALF, 1 - u // HALF, i * 2 + u // HALF + 2)

            with dve.Fori(1, CHECK_TURN) as i:
                turn(i)
            n = done(dve.tensor_scalar(outside[:, :], rel[:, :], 0.0, None, ALU.is_lt))
            dve.wait_ge(chain, n)
            n = done(dve.scalar_tensor_tensor(out=outside[:, :], in0=rel[:, :], scalar=float(W), in1=outside[:, :],
                                              op0=ALU.is_ge, op1=ALU.max))
            dve.wait_ge(chain, n)
            dve.tensor_reduce(group_out[:, :], outside[:, :].rearrange("p (g t) -> p g t", t=TPG), AX_X, ALU.max
                              ).then_inc(outside_ready, 1)
            dve.wait_ge(outside_counted, 1)
            n = done(dve.tensor_reduce(n_out_f[:, :], pB2[1][0:1, 0:GROUPS], AX_X, ALU.add))
            dve.tensor_copy(n_out[:, :], pB2[1][0:1, 0:GROUPS]).then_inc(counts_ready, 1)
            dve.wait_ge(chain, n)
            dve.tensor_copy(n_out_all[:, :], n_out_f[:, :]).then_inc(counts_ready, 1)

            left = edges_left(dve)
            with dve.Fori(CHECK_TURN, TURNS) as i:
                turn(i)
            for g in range(TURNS * RING + LEAD, GROUPS):
                make_scatter(g, g % 4, g % 2, g + RING - 3)
            last_bases = {g: first_node(g) for g in range(TURNS * RING, GROUPS)}
            for g in range(TURNS * RING - HALF, GROUPS):
                add_window(g, g % HALF, g // HALF % 2, g // HALF + 3, last_bases.get(g))
            dve.wait_ge(added, 2 * GROUPS + 4 * HALF)
            with dve.If(left > 0):
                dve.tensor_copy(rel[:, :], dst_i[:, :]).then_inc(left_dst, 1)
                dve.wait_ge(left_dst, 1)
                dve.scalar_tensor_tensor(out=rel[:, :], in0=rel[:, :], scalar=1.0, in1=outside[:, :],
                                         op0=ALU.add, op1=ALU.mult).then_inc(left_dst, 1)
                dve.wait_ge(left_dst, 2)
                dve.tensor_scalar(rel[:, :], rel[:, :], -1.0, None, ALU.add).then_inc(left_dst, 1)
                dve.wait_ge(left_dst, 3)
                with dve.Fori(0, GROUPS) as g:
                    with dve.If(group_left(dve, g) > 0):
                        with dve.Fori(0, WINDOWS) as j:
                            dve.tensor_tensor(onehot[:, 0, :, :],
                                              iota_w[:, :].unsqueeze(1).to_broadcast([P, TPG, W]),
                                              rel[:, bass.ds(g * TPG, TPG)].unsqueeze(2).to_broadcast([P, TPG, W]),
                                              ALU.is_equal).then_inc(left_onehot, 1)
                            dve.wait_ge(left_onehot, 1)
                            dve.sem_inc(left_onehot, -1)
                            dve.tensor_tensor(
                                scat[:, 0, :, :, :], onehot[:, 0, :, :].unsqueeze(2).to_broadcast([P, TPG, 4, W]),
                                sh_sb[:, bass.ds(g * TPG, TPG), :].unsqueeze(3).to_broadcast([P, TPG, 4, W]),
                                ALU.mult).then_inc(left_scat, 1)
                            dve.tensor_scalar(rel[:, bass.ds(g * TPG, TPG)], rel[:, bass.ds(g * TPG, TPG)],
                                              -float(W), None, ALU.add).then_inc(left_added, 1)
                            dve.wait_ge(left_mapped, 1)
                            dve.sem_inc(left_mapped, -1)
                            here = bass.ds(j * W, W)
                            dve.tensor_tensor(acc1[:, here], acc1[:, here], pB1[0][:, 0:W], ALU.add
                                              ).then_inc(left_added, 1)
                            dve.tensor_tensor(acc2[:, here], acc2[:, here], pB2[0][0:F2, 0:W], ALU.add
                                              ).then_inc(left_added, 1)
                            dve.wait_ge(left_added, 3)
                            dve.sem_inc(left_added, -3)
            dve.sem_inc(sums_ready, 1)

            for n, j in enumerate(range(0, PER, BLK)):
                e = min(j + BLK, PER)
                dve.wait_ge(turned, n + 1)
                dve.scalar_tensor_tensor(out=xh[:, j:e, :], in0=banks[n % 8][0:NP, 0:(e - j) * D].rearrange(
                    "p (j d) -> p j d", d=D), scalar=0.0, in1=xh[:, j:e, :], op0=ALU.max, op1=ALU.add
                ).then_inc(finished, 1)

        @block.tensor
        def _(pe):
            pe.sem_inc(agg_done, RING)
            pe.sem_inc(mapped, 2)
            pe.sem_inc(agg_copied, 2)
            pe.wait_ge(z_ready, 16)
            for blk in range(4):
                kk, w = (MUL0, ws_s) if blk == 0 else (MUL1, wv_s)
                cols = slice(0, MUL0) if blk == 0 else slice(MUL0 + blk - 1, D, 3)
                for k in range(4):
                    nc.tensor.matmul(banks[k][:, cols], z[0:kk, blk, k, 0:F1], w[:, :], start=True, stop=True)
                    last = nc.tensor.matmul(banks[4][F2 * k:F2 * k + F2, cols], z[0:kk, blk, k, F1:D], w[:, :],
                                            start=True, stop=True, tile_position=(0, F2 * k))
            last.then_inc(L_product, 1)
            pe.wait_ge(base_ready, 2)
            nc.tensor.matmul(pB1[1][:, 0:GROUPS], ones_row[:, :], base_f[:, :], start=True, stop=True
                             ).then_inc(base_spread, 1)
            pe.wait_ge(base_spread, 2)
            pe.wait_ge(L_ready, 5)

            def sum_window(slot, s, b, m):
                nodes = slice(m * W, (m + 1) * W)
                for t in range(TPG):
                    nc.tensor.matmul(half_view(pA1[b])[:, :, nodes], rows[:, slot, t, 0:F1], scat[:, s, t, :, :],
                                     start=(t == 0), stop=(t == TPG - 1))
                for t in range(TPG):
                    for k in range(4):
                        last = nc.tensor.matmul(pA2[b][F2 * k:F2 * k + F2, nodes], rows[:, slot, t, F1:D],
                                                scat[:, s, t, k, :], start=(t == 0), stop=(t == TPG - 1),
                                                tile_position=(0, F2 * k))
                return last

            def map_sums(b, n):
                for o, cols in ((pB1[b][:, 0:n], slice(0, F1)), (pB2[b][0:F2, 0:n], slice(F1, D))):
                    for k in range(4):
                        nc.tensor.matmul(o, L1[:, k, cols], agg1[:, b, k, 0:n], start=(k == 0), stop=False)
                    last = nc.tensor.matmul(o, L2[:, cols], agg2[:, b, 0:n], start=False, stop=True)
                return last

            def aggregate(slot, landed, scattered, by=None):
                pe.wait_ge(by if by is not None else gathered[slot], landed)
                pe.wait_ge(scat_ready, scattered)
                pe.sem_inc(slot_seen_free, 1)
                sum_window(slot, slot % 4, slot // HALF, slot % HALF).then_inc(agg_done, 1)

            def map_half(b, copied, free, groups=HALF):
                pe.wait_ge(agg_copied, copied)
                pe.wait_ge(added, free)
                pe.sem_inc(slot_seen_free, 1)
                map_sums(b, groups * W).then_inc(mapped, 1)

            for g in range(RING):
                aggregate(g, g * TPG + TPG, g + 1, rows_normed)
                if g == HALF:
                    map_half(0, 4, 2 * HALF)

            def turn(i):
                for u in range(RING):
                    if u % HALF == 0:
                        pe.wait_ge(agg_copied, i * 4 + u // HALF * 2)
                        pe.sem_inc(slot_seen_free, 1)
                    aggregate(u, i * (16 * TPG) + 16 * TPG, i * RING + u + 1)
                    if u % HALF == 0:
                        map_half(1 - u // HALF, i * 4 + u // HALF * 2 + 2,
                                 i * (4 * HALF) + u // HALF * (2 * HALF))

            with pe.Fori(1, CHECK_TURN) as i:
                turn(i)
            pe.wait_ge(outside_ready, 1)
            nc.tensor.matmul(pB2[1][0:1, 0:GROUPS], ones_col[:, :], group_out[:, :], start=True, stop=True
                             ).then_inc(outside_counted, 1)
            left = edges_left(pe)
            with pe.Fori(CHECK_TURN, TURNS) as i:
                turn(i)
            pe.wait_ge(agg_copied, 2 * LAST_HALF)
            for u in range(TAIL):
                aggregate(u, (TURNS + 1) * 16 * TPG, TURNS * RING + u + 1)
                if u == 0:
                    map_half(1, 2 * LAST_HALF + 2, 2 * HALF * LAST_HALF)
            map_half(0, 2 * LAST_HALF + 4, 2 * HALF * (LAST_HALF + 1), TAIL)
            with pe.If(left > 0):
                pe.wait_ge(added, 2 * GROUPS + 4 * HALF)
                pe.sem_inc(left_group_done, 1)
                with pe.Fori(0, GROUPS) as g:
                    pe.wait_ge(left_rows, g * (16 * TPG) + 16 * TPG)
                    with pe.If(group_left(pe, g) > 0):
                        with pe.Fori(0, WINDOWS) as _j:
                            pe.wait_ge(left_scat, 1)
                            pe.sem_inc(left_scat, -1)
                            sum_window(0, 0, 0, 0).then_inc(left_agg, 1)
                            pe.wait_ge(left_copied, 2)
                            pe.sem_inc(left_copied, -2)
                            map_sums(0, W).then_inc(left_mapped, 1)
                    pe.sem_inc(left_group_done, 1)

            pe.wait_ge(sums_ready, 1)
            pe.wait_ge(const_made, 3)
            for n, j in enumerate(range(0, PER, BLK)):
                if n >= 8:
                    pe.wait_ge(finished, n - 7)
                for q in range(j, min(j + BLK, PER)):
                    o = banks[n % 8][0:NP, (q - j) * D:(q - j + 1) * D]
                    nc.tensor.transpose(o[:, 0:F1], acc1[:, q:q + (NP - 1) * PER + 1:PER], ident[:, :])
                    last = nc.tensor.transpose(o[:, F1:D], acc2[:, q:q + (NP - 1) * PER + 1:PER], ident[0:F2, 0:F2])
                last.then_inc(turned, 1)


_INS = ["x", "src", "dst", "sh", "w1t", "w2t", "w3t", "w4t", "w5t", "ws", "wv"]


def kernel(x, src, dst, edge_attr_4, L0_gnn_W1, L0_gnn_W2, L0_gnn_W3, L0_gnn_W4, L0_gnn_W5, L0_gnn_Ws, L0_gnn_Wv):
    import numpy as _np
    import concourse.bacc as _bacc
    from concourse import mybir as _mybir
    from concourse.bass_utils import run_bass_kernel_spmd as _run

    pad = TILES * P - EDGES
    src_t = _np.pad(_np.asarray(src), (0, pad), mode="edge").reshape(TILES, P).T
    dst_t = _np.pad(_np.asarray(dst), (0, pad), mode="edge").reshape(TILES, P).T
    sh_t = _np.pad(_np.asarray(edge_attr_4), ((0, pad), (0, 0))).reshape(TILES, P, 4).transpose(1, 0, 2).reshape(
        P, TILES * 4)
    values = [x, src_t, dst_t, sh_t, _np.asarray(L0_gnn_W1).T, _np.asarray(L0_gnn_W2).T, _np.asarray(L0_gnn_W3).T,
              _np.asarray(L0_gnn_W4).T, _np.asarray(L0_gnn_W5).T, L0_gnn_Ws, L0_gnn_Wv]

    nc = _bacc.Bacc("TRN2", target_bir_lowering=False, num_devices=1)
    arrays, args = {}, []
    for name, value in zip(_INS, values):
        a = _np.ascontiguousarray(value)
        arrays[f"in_{name}_dram"] = a
        args.append(nc.dram_tensor(f"in_{name}_dram", a.shape, _mybir.dt.from_np(a.dtype), kind="ExternalInput").ap())
    args.append(nc.dram_tensor("table_dram", (NODES, D), F32, kind="Internal").ap())
    args.append(nc.dram_tensor("out_0_dram", (NODES, D), F32, kind="ExternalOutput").ap())
    gnn_kernel(nc, *args)
    r = _run(nc, [arrays], core_ids=[0])
    return r.results[0]["out_0_dram"]
```

```python
from contextlib import ExitStack

import concourse.bass as bass
from concourse import mybir

F32 = mybir.dt.float32
I32 = mybir.dt.int32
ALU = mybir.AluOpType
ACT = mybir.ActivationFunctionType
AX_X = mybir.AxisListType.X

NODES = 6250
MUL0, MUL1 = 64, 32
D = MUL0 + 3 * MUL1
EDGES = 206250
EPS = 1e-5

C0 = (MUL0 + MUL1) ** -0.5
C1 = (3.0 / (MUL0 + 2 * MUL1)) ** 0.5
INV3 = 3.0 ** -0.5
INV6 = 6.0 ** -0.5
LIN_S = MUL0 ** -0.5
LIN_V = MUL1 ** -0.5

P = 128
TPG = 4
W = 24
GROUPS = -(-EDGES // (P * TPG))
TILES = GROUPS * TPG
RING = 8
HALF = RING // 2
TURNS = (GROUPS - 1) // RING
TAIL = GROUPS - TURNS * RING
LAST_HALF = 2 * TURNS
CHECK_TURN = 4
PAIRS = RING // 2
SH_FIRST = 3 * RING * TPG
AHEAD = 4
LEAD = 2
assert LEAD <= TAIL <= HALF

BLOCKS = -(-NODES // P)
FULL = NODES // P
LAST_ROWS = NODES - FULL * P
CHUNKS = 7
CH = BLOCKS // CHUNKS
assert CHUNKS * CH == BLOCKS == FULL + 1
H_BUFS = CHUNKS - 1
STEP = 3
FIN_BANKS = 4
EARLY_TURN = 47
EARLY = 44
EARLY_STEPS = -(-EARLY // STEP)
STEPS = EARLY_STEPS + -(-(BLOCKS - EARLY) // STEP)
WINDOWS = -(-NODES // W)
COLS = WINDOWS * W + W
F1, F2 = P, D - P


def gnn_kernel(nc: bass.Bass, x, src, dst, sh, w1t, w2t, w3t, w4t, w5t, ws, wv, table, out):
    def node_parts(dram, tile, j, e, at=0):
        full = min(e, FULL)
        parts = [(dram[j * P:full * P, :].rearrange("(j p) d -> p j d", p=P), tile[:, at:at + full - j, :])]
        if e > FULL:
            parts.append((dram[FULL * P:NODES, :], tile[0:LAST_ROWS, at + FULL - j, :]))
        return parts

    def finish_steps(first, last):
        n = 0 if first == 0 else EARLY_STEPS
        return [(n + m, j, min(j + STEP, last)) for m, j in enumerate(range(first, last, STEP))]

    with ExitStack() as ctx:
        def sb(name, shape, dt=F32):
            return ctx.enter_context(nc.sbuf_tensor(name, shape, dt))

        def ps(name, shape):
            return ctx.enter_context(nc.psum_tensor(name, shape, F32))

        def sem(name):
            return ctx.enter_context(nc.semaphore(name))

        xh = sb("xh", [P, BLOCKS, D])
        h = sb("h", [P, H_BUFS, CH, D])
        stats = sb("stats", [P, BLOCKS, 6])
        mv = sb("mv", [P, BLOCKS, 2])
        std = sb("std", [P, BLOCKS])
        rstd = sb("rstd", [P, BLOCKS])
        shift = sb("shift", [P, BLOCKS])
        eps_t = sb("eps_t", [P, 1])
        root_eps = sb("root_eps", [P, 1])
        acc1 = sb("acc1", [F1, COLS])
        acc2 = sb("acc2", [F2, COLS])
        dst_i = sb("dst_i", [P, TILES], I32)
        rel = sb("rel", [P, TILES])
        sh_sb = sb("sh_sb", [P, TILES, 4])
        idx = [sb(f"idx{k}", [P, HALF * TPG], I32) for k in range(2)]
        idx_first = [sb(f"idx_first{k}", [P, HALF * TPG], I32) for k in range(2)]
        base_f = sb("base_f", [1, GROUPS])
        base_i = sb("base_i", [1, GROUPS], I32)
        outside = sb("outside", [P, TILES])
        group_out = sb("group_out", [P, GROUPS])
        n_out = sb("n_out", [1, GROUPS], I32)
        n_out_f = sb("n_out_f", [1, 1])
        falls = group_out[0:1, :]
        n_falls = sb("n_falls", [1, 1])
        late = sb("late", [1, 1])
        held_f = sb("held_f", [1, 1])
        held = sb("held", [1, 1], I32)
        n_out_all = sb("n_out_all", [1, 1], I32)
        rows = sb("rows", [P, RING, TPG, D])
        row_stats = sb("row_stats", [P, PAIRS, 2 * TPG, 6])
        row_mv = sb("row_mv", [P, PAIRS, 2 * TPG, 2])
        row_std = sb("row_std", [P, PAIRS, 2 * TPG])
        row_rstd = sb("row_rstd", [P, PAIRS, 2 * TPG])
        row_shift = sb("row_shift", [P, PAIRS, 2 * TPG])
        onehot = sb("onehot", [P, 2, TPG, W])
        scat = sb("scat", [P, 4, TPG, 4, W])
        agg1 = sb("agg1", [F1, 2, 4, HALF * W])
        agg2 = sb("agg2", [P, 2, HALF * W])
        iota_i = sb("iota_i", [P, W], I32)
        iota_w = sb("iota_w", [P, W])
        ones_row = sb("ones_row", [1, P])
        ones_col = sb("ones_col", [P, 1])
        ident = sb("ident", [P, P])
        w1s = sb("w1s", [MUL0, MUL0])
        w2s = sb("w2s", [MUL0, MUL1])
        w3s = sb("w3s", [MUL1, MUL0])
        w4s = sb("w4s", [MUL1, MUL1])
        w5s = sb("w5s", [MUL1, MUL1])
        ws_s = sb("ws_s", [MUL0, MUL0])
        wv_s = sb("wv_s", [MUL1, MUL1])
        z = sb("z", [MUL0, 4, 4, D])
        L1 = sb("L1", [F1, 4, D])
        L2 = sb("L2", [P, D])

        pA = [ps(f"pA{k}", [P, 512]) for k in range(2)]
        pA1 = [t[:, 0:4 * HALF * W] for t in pA]
        pA2 = [t[:, 4 * HALF * W:5 * HALF * W] for t in pA]
        pB = [ps(f"pB{k}", [P, 512]) for k in range(2)]
        pB1 = [t[:, 0:HALF * W] for t in pB]
        pB2 = [t[:, HALF * W:2 * HALF * W] for t in pB]
        fin = [ps(f"fin{k}", [P, 512]) for k in range(FIN_BANKS)]

        x_loaded = [sem(f"x_loaded{c}") for c in range(CHUNKS)]
        dst_loaded = sem("dst_loaded")
        sh_loaded = [sem(f"sh_loaded{k}") for k in range(2)]
        weights_loaded = sem("weights_loaded")
        const_made = sem("const_made")
        filled = sem("filled")
        chain = sem("chain")
        var_ready = sem("var_ready")
        std_ready = sem("std_ready")
        norm_ready = sem("norm_ready")
        h_ready = sem("h_ready")
        xh_ready = sem("xh_ready")
        h_stored = [sem(f"h_stored{c}") for c in range(CHUNKS)]
        base_ready = sem("base_ready")
        base_spread = sem("base_spread")
        z_ready = sem("z_ready")
        L_product = sem("L_product")
        L_ready = sem("L_ready")
        idx_first_loaded = [sem(f"idx_first_loaded{k}") for k in range(2)]
        idx_loaded = [sem(f"idx_loaded{k}") for k in range(2)]
        gathered = [sem(f"gathered{k}") for k in range(RING)]
        slot_seen_free = sem("slot_seen_free")
        onehot_made = sem("onehot_made")
        scat_ready = sem("scat_ready")
        agg_done = sem("agg_done")
        row_var_ready = sem("row_var_ready")
        row_std_ready = sem("row_std_ready")
        row_norm_ready = sem("row_norm_ready")
        rows_normed = sem("rows_normed")
        zeroed = sem("zeroed")
        acc2_zeroed = sem("acc2_zeroed")
        agg_copied = sem("agg_copied")
        mapped = sem("mapped")
        added = sem("added")
        outside_ready = sem("outside_ready")
        outside_counted = sem("outside_counted")
        counts_ready = sem("counts_ready")
        sums_ready = sem("sums_ready")
        left_dst = sem("left_dst")
        left_idx = sem("left_idx")
        left_rows = sem("left_rows")
        left_seen = sem("left_seen")
        left_group_done = sem("left_group_done")
        left_onehot = sem("left_onehot")
        left_scat = sem("left_scat")
        left_agg = sem("left_agg")
        left_copied = sem("left_copied")
        left_mapped = sem("left_mapped")
        left_added = sem("left_added")
        turned = sem("turned")
        finished = sem("finished")
        out_stored = sem("out_stored")

        block = ctx.enter_context(nc.Block())

        def half_view(bank):
            return bank[:, 0:4 * HALF * W].rearrange("p (k n) -> p k n", k=4)

        def edges_left(eng):
            eng.wait_ge(counts_ready, 3)
            return eng.value_load(n_out_all[0:1, 0:1], min_val=0, max_val=P * GROUPS)

        def early_held(eng):
            eng.wait_ge(counts_ready, 3)
            return eng.value_load(held[0:1, 0:1], min_val=0, max_val=(P + 1) * GROUPS + 1)

        def group_left(eng, g):
            return eng.value_load(n_out[0:1, bass.ds(g, 1)], min_val=0, max_val=P)

        @block.sync
        def _(sp):
            for k in range(2):
                sp.dma_start(idx_first[k][:, :], src[:, k * HALF * TPG:(k + 1) * HALF * TPG]
                             ).then_inc(idx_first_loaded[k], 16)
            for c in range(CHUNKS):
                if c == CHUNKS - 1:
                    sp.wait_ge(filled, 4)
                for of, to in node_parts(x, xh, c * CH, (c + 1) * CH, c * CH):
                    sp.dma_start(to, of).then_inc(x_loaded[c], 16)
            for t, w in ((w1s, w1t), (w2s, w2t), (w3s, w3t), (w4s, w4t), (w5s, w5t), (ws_s, ws), (wv_s, wv)):
                sp.dma_start(t[:, :], w).then_inc(weights_loaded, 16)
            for k in range(2):
                at = (RING + k * HALF) * TPG
                sp.dma_start(idx[k][:, :], src[:, at:at + HALF * TPG]).then_inc(idx_loaded[k], 16)
            sp.dma_start(dst_i[:, :], dst).then_inc(dst_loaded, 16)
            sh_tiles = sh_sb[:, :, :].rearrange("p t k -> p (t k)")
            sp.dma_start(sh_tiles[:, 0:4 * SH_FIRST], sh[:, 0:4 * SH_FIRST]).then_inc(sh_loaded[0], 16)
            sp.wait_ge(zeroed, 1)
            sp.dma_start(acc2[:, :], acc1[0:F2, :]).then_inc(acc2_zeroed, 16)
            for c in range(CHUNKS):
                sp.wait_ge(h_ready, CH * (c + 1))
                for to, of in node_parts(table, h[:, c % H_BUFS, :, :], c * CH, (c + 1) * CH):
                    sp.dma_start(to, of).then_inc(h_stored[c], 16)
            sp.dma_start(sh_tiles[:, 4 * SH_FIRST:], sh[:, 4 * SH_FIRST:]).then_inc(sh_loaded[1], 16)
            with sp.Fori(2, TURNS) as i:
                for k in range(2):
                    for u in range(k * HALF, (k + 1) * HALF):
                        sp.wait_ge(gathered[u], i * (16 * TPG))
                    sp.dma_start(idx[k][:, :], src[:, bass.ds(i * (RING * TPG) + k * HALF * TPG, HALF * TPG)]
                                 ).then_inc(idx_loaded[k], 16)
            for u in range(HALF):
                sp.wait_ge(gathered[u], TURNS * (16 * TPG))
            sp.dma_start(idx[0][:, 0:TAIL * TPG], src[:, TURNS * RING * TPG:TILES]).then_inc(idx_loaded[0], 16)
            with sp.If(edges_left(sp) > 0):
                sp.wait_ge(agg_done, GROUPS + RING)
                with sp.Fori(0, GROUPS) as g:
                    sp.wait_ge(left_group_done, g + 1)
                    sp.dma_start(idx[0][:, 0:TPG], src[:, bass.ds(g * TPG, TPG)]).then_inc(left_idx, 16)

        @block.gpsimd
        def _(pool):
            pool.iota(iota_i[:, :], [[1, W]], base=0, channel_multiplier=0).then_inc(const_made, 1)
            pool.memset(ident[:, :], 0.0).then_inc(const_made, 1)
            pool.wait_ge(const_made, 2)
            pool.affine_select(out=ident[:, :], in_=ident[:, :], compare_op=ALU.not_equal, fill=1.0, base=0,
                               pattern=[[-1, P]], channel_multiplier=1).then_inc(const_made, 1)

            def gather(slot, k, col, of=table, by=idx):
                pool.indirect_dma_start(
                    out=rows[:, slot, k, :], out_offset=None, in_=of,
                    in_offset=bass.IndirectOffsetOnAxis(ap=by[slot // HALF][:, col:col + 1], axis=0)
                ).then_inc(gathered[slot], 16)

            for u in range(RING):
                if u % HALF == 0:
                    pool.wait_ge(idx_first_loaded[u // HALF], 16)
                for k in range(TPG):
                    gather(u, k, (u % HALF) * TPG + k, x, idx_first)
            for c in range(CHUNKS):
                pool.wait_ge(h_stored[c], 16 * (1 + c // (CHUNKS - 1)))
            with pool.Fori(1, TURNS) as i:
                for u in range(RING):
                    if u % HALF == 0:
                        pool.wait_ge(idx_loaded[u // HALF], i * 16)
                    pool.wait_ge(agg_done, i * RING + u + 1)
                    pool.sem_inc(slot_seen_free, 1)
                    for k in range(TPG):
                        gather(u, k, (u % HALF) * TPG + k)
            pool.wait_ge(idx_loaded[0], 16 * TURNS)
            for u in range(TAIL):
                pool.wait_ge(agg_done, TURNS * RING + u + 1)
                for k in range(TPG):
                    gather(u, k, u * TPG + k)
            with pool.If(edges_left(pool) > 0):
                pool.wait_ge(agg_done, GROUPS + RING)
                with pool.Fori(0, GROUPS) as g:
                    pool.wait_ge(left_idx, g * 16 + 16)
                    pool.sem_inc(left_seen, 1)
                    for k in range(TPG):
                        pool.indirect_dma_start(
                            out=rows[:, 0, k, :], out_offset=None, in_=table,
                            in_offset=bass.IndirectOffsetOnAxis(ap=idx[0][:, k:k + 1], axis=0)
                        ).then_inc(left_rows, 16)

        @block.scalar
        def _(act):
            act.wait_ge(filled, 1)
            nc.scalar.activation(root_eps[:, :], eps_t[:, :], ACT.Sqrt)
            act.wait_ge(filled, 2)
            nc.scalar.activation(acc1[:, :], ones_col[:, 0:1].to_broadcast([P, COLS]), ACT.Copy, scale=0.0
                                 ).then_inc(zeroed, 1)

            def take_root(c):
                js = slice(c * CH, (c + 1) * CH)
                act.wait_ge(var_ready, c + 1)
                nc.scalar.activation(std[:, js], mv[:, js, 1], ACT.Sqrt, bias=eps_t[:, 0:1]).then_inc(std_ready, 1)

            def copy_sums(b, done, used, groups=HALF):
                act.wait_ge(agg_done, done)
                act.wait_ge(mapped, used)
                act.sem_inc(slot_seen_free, 1)
                n = groups * W
                nc.scalar.copy(agg1[:, b, :, 0:n], half_view(pA1[b])[:, :, 0:n]).then_inc(agg_copied, 1)
                nc.scalar.copy(agg2[:, b, 0:n], pA2[b][:, 0:n]).then_inc(agg_copied, 1)

            def row_root(q):
                act.wait_ge(row_var_ready, q + 1)
                nc.scalar.activation(row_std[:, q, :], row_mv[:, q, :, 1], ACT.Sqrt, bias=eps_t[:, 0:1]
                                     ).then_inc(row_std_ready, 1)

            def norm_rows(q):
                act.wait_ge(row_norm_ready, q + 1)
                for n in range(2 * TPG):
                    r = rows[:, 2 * q + n // TPG, n % TPG, :]
                    nc.scalar.activation(r, r, ACT.Relu, bias=row_shift[:, q, n:n + 1],
                                         scale=row_rstd[:, q, n:n + 1]).then_inc(rows_normed, 1)

            take_root(0)
            for c in range(CHUNKS):
                act.wait_ge(norm_ready, c + 1)
                if c >= H_BUFS:
                    act.wait_ge(h_stored[c - H_BUFS], 16)
                    act.wait_ge(xh_ready, c - H_BUFS + 1)
                for j in range(c * CH, (c + 1) * CH):
                    nc.scalar.activation(h[:, c % H_BUFS, j - c * CH, :], xh[:, j, :], ACT.Relu,
                                         bias=shift[:, j:j + 1], scale=rstd[:, j:j + 1]).then_inc(h_ready, 1)
                    if j == (c + 1) * CH - AHEAD and c + 1 < CHUNKS:
                        take_root(c + 1)

            row_root(0)
            for q in range(PAIRS + 1):
                if q < PAIRS:
                    norm_rows(q)
                if q + 1 < PAIRS:
                    row_root(q + 1)
                if q == 0:
                    act.wait_ge(L_product, 1)
                    for k in range(4):
                        nc.scalar.copy(L1[:, k, :], fin[k][:, 0:D]).then_inc(L_ready, 1)
                    nc.scalar.copy(L2[:, :], pB[1][:, 0:D]).then_inc(L_ready, 1)
                if q in (2, 4):
                    hf = q // 2 - 1
                    copy_sums(hf, (hf + 1) * HALF + RING, hf + 1)

            def store(first, last):
                for n, j, e in finish_steps(first, last):
                    act.wait_ge(finished, n + 1)
                    for to, of in node_parts(out, xh, j, e, j):
                        act.dma_start(to, of).then_inc(out_stored, 16)

            with act.Fori(1, EARLY_TURN) as i:
                for hf in range(2):
                    copy_sums(hf, i * RING + (hf + 1) * HALF + RING, i * 2 + hf + 1)
            hold = early_held(act)
            with act.If(hold == 0):
                store(0, EARLY)
            with act.Fori(EARLY_TURN, TURNS) as i:
                for hf in range(2):
                    copy_sums(hf, i * RING + (hf + 1) * HALF + RING, i * 2 + hf + 1)
            copy_sums(0, GROUPS + RING, LAST_HALF + 1, TAIL)
            with act.If(edges_left(act) > 0):
                act.wait_ge(mapped, LAST_HALF + 1 + 2)
                with act.Fori(0, GROUPS) as g:
                    with act.If(group_left(act, g) > 0):
                        with act.Fori(0, WINDOWS) as _j:
                            act.wait_ge(left_agg, 1)
                            act.sem_inc(left_agg, -1)
                            nc.scalar.copy(agg1[:, 0, :, 0:W], half_view(pA1[0])[:, :, 0:W]
                                           ).then_inc(left_copied, 1)
                            nc.scalar.copy(agg2[:, 0, 0:W], pA2[0][:, 0:W]).then_inc(left_copied, 1)
            with act.If(hold > 0):
                store(0, EARLY)
            store(EARLY, BLOCKS)
            act.wait_ge(out_stored, 16 * (STEPS + 1))

        @block.vector
        def _(dve):
            steps = [0]

            def done(ins):
                steps[0] += 1
                ins.then_inc(chain, 1)
                return steps[0]

            dve.memset(eps_t[:, :], EPS).then_inc(filled, 1)
            dve.memset(ones_row[:, :], 1.0).then_inc(base_ready, 1)
            dve.memset(ones_col[:, :], 1.0).then_inc(filled, 1)
            dve.memset(z[:, :, :, :], 0.0).then_inc(filled, 1)
            dve.memset(xh[:, FULL, :], 0.0).then_inc(filled, 1)

            def node_sums(c):
                dve.wait_ge(x_loaded[c], 16 * (1 + c // (CHUNKS - 1)))
                for j in range(c * CH, (c + 1) * CH):
                    n = done(dve.bn_stats(stats[:, j, :], xh[:, j, :]))
                    if c > 0 and j == c * CH + CH // 2:
                        node_scale(c - 1)
                dve.wait_ge(chain, n)
                for j in range(c * CH, (c + 1) * CH):
                    ins = dve.bn_aggr(mv[:, j, :], stats[:, j, :])
                    n = done(ins)
                dve.wait_ge(chain, n)
                dve.sem_inc(var_ready, 1)

            def node_scale(c):
                js = slice(c * CH, (c + 1) * CH)
                dve.wait_ge(std_ready, c + 1)
                dve.wait_ge(chain, done(dve.reciprocal(rstd[:, js], std[:, js])))
                dve.scalar_tensor_tensor(out=shift[:, js], in0=mv[:, js, 0], scalar=-1.0, in1=rstd[:, js],
                                         op0=ALU.mult, op1=ALU.mult).then_inc(norm_ready, 1)

            def add_h(c):
                js = slice(c * CH, (c + 1) * CH)
                dve.wait_ge(h_ready, CH * (c + 1))
                dve.tensor_tensor(xh[:, js, :], xh[:, js, :], h[:, c % H_BUFS, :, :], ALU.add).then_inc(xh_ready, 1)

            def vec(a):
                return slice(MUL0 + a, D, 3)

            def put(block_, k, cols, w, scale):
                dve.tensor_scalar(z[0:w.shape[0], block_, k, cols], w[:, :], scale, None, ALU.mult
                                  ).then_inc(z_ready, 1)

            def put_weights():
                dve.wait_ge(weights_loaded, 16 * 7)
                dve.wait_ge(filled, 3)
                put(0, 0, slice(0, MUL0), w1s, C0 * LIN_S)
                for a in range(3):
                    put(0, 1 + a, vec(a), w2s, C0 * INV3 * LIN_S)
                    put(1 + a, 1 + a, slice(0, MUL0), w3s, C1 * INV3 * LIN_V)
                    put(1 + a, 0, vec(a), w4s, C1 * INV3 * LIN_V)
                    for b in range(3):
                        if a != b:
                            sign = 1.0 if (b - a) % 3 == 1 else -1.0
                            put(1 + 3 - a - b, 1 + b, vec(a), w5s, sign * C1 * INV6 * LIN_V)

            for c in range(CHUNKS):
                node_sums(c)
                if c == 3:
                    put_weights()
            node_scale(CHUNKS - 1)
            dve.wait_ge(dst_loaded, 16)
            dve.tensor_copy(base_f[:, :], dst_i[0:1, 0:TILES:TPG]).then_inc(base_ready, 1)
            for c in range(CHUNKS - H_BUFS):
                add_h(c)

            def make_scatter(g, s, o, used):
                dve.tensor_tensor(onehot[:, o, :, :], iota_w[:, :].unsqueeze(1).to_broadcast([P, TPG, W]),
                                  rel[:, bass.ds(g * TPG, TPG)].unsqueeze(2).to_broadcast([P, TPG, W]),
                                  ALU.is_equal).then_inc(onehot_made, 1)
                dve.wait_ge(onehot_made, g + 1)
                dve.wait_ge(agg_done, used)
                dve.tensor_tensor(scat[:, s, :, :, :], onehot[:, o, :, :].unsqueeze(2).to_broadcast([P, TPG, 4, W]),
                                  sh_sb[:, bass.ds(g * TPG, TPG), :].unsqueeze(3).to_broadcast([P, TPG, 4, W]),
                                  ALU.mult).then_inc(scat_ready, 1)

            def first_node(g):
                return dve.value_load(base_i[0:1, bass.ds(g, 1)], min_val=0, max_val=NODES - 1)

            def add_window(g, m, b, mapped_halves, base=None):
                if base is None:
                    base = first_node(g)
                dve.wait_ge(mapped, mapped_halves)
                dve.wait_ge(added, g * 2 + 4 * HALF)
                dve.tensor_tensor(acc1[:, bass.ds(base, W)], acc1[:, bass.ds(base, W)],
                                  pB1[b][:, m * W:(m + 1) * W], ALU.add).then_inc(added, 1)
                dve.tensor_tensor(acc2[:, bass.ds(base, W)], acc2[:, bass.ds(base, W)],
                                  pB2[b][0:F2, m * W:(m + 1) * W], ALU.add).then_inc(added, 1)

            def row_sums(q):
                for g in (2 * q, 2 * q + 1):
                    dve.wait_ge(gathered[g], 16 * TPG)
                for m in range(2 * TPG):
                    n = done(dve.bn_stats(row_stats[:, q, m, :], rows[:, 2 * q + m // TPG, m % TPG, :]))
                dve.wait_ge(chain, n)
                for m in range(2 * TPG):
                    ins = dve.bn_aggr(row_mv[:, q, m, :], row_stats[:, q, m, :])
                    n = done(ins)
                dve.wait_ge(chain, n)
                dve.sem_inc(row_var_ready, 1)

            def row_scale(q):
                dve.wait_ge(row_std_ready, q + 1)
                dve.wait_ge(chain, done(dve.reciprocal(row_rstd[:, q, :], row_std[:, q, :])))
                dve.scalar_tensor_tensor(out=row_shift[:, q, :], in0=row_mv[:, q, :, 0], scalar=-1.0,
                                         in1=row_rstd[:, q, :], op0=ALU.mult, op1=ALU.mult
                                         ).then_inc(row_norm_ready, 1)

            dve.sem_inc(added, 4 * HALF)
            row_sums(0)
            done(dve.tensor_copy(rel[:, :], dst_i[:, :]))
            row_scale(0)
            dve.wait_ge(const_made, 3)
            n = done(dve.tensor_copy(iota_w[:, :], iota_i[:, :]))
            dve.wait_ge(chain, n)
            dve.wait_ge(base_spread, 1)
            rel_v = rel[:, :].rearrange("p (g t) -> p g t", t=TPG)
            n = done(dve.tensor_tensor(rel_v, rel_v, pA[0][:, 0:GROUPS].unsqueeze(2).to_broadcast([P, GROUPS, TPG]),
                                       ALU.subtract))
            dve.wait_ge(chain, n)
            dve.sem_inc(base_spread, 1)
            dve.wait_ge(sh_loaded[0], 16)
            for g in range(LEAD):
                make_scatter(g, g, g % 2, RING)
            for q in range(1, PAIRS + 1):
                if q < PAIRS:
                    row_sums(q)
                for g in (2 * q, 2 * q + 1):
                    make_scatter(g, g % 4, g % 2, g + RING - 3)
                if q < PAIRS:
                    row_scale(q)
                if q == 2:
                    dve.wait_ge(chain, done(dve.tensor_copy(base_i[:, :], dst_i[0:1, 0:TILES:TPG])))
                    dve.wait_ge(zeroed, 1)
                    dve.wait_ge(acc2_zeroed, 16)
                if q > 2:
                    for g in (2 * q - 6, 2 * q - 5):
                        add_window(g, g, 0, 3)
            dve.wait_ge(sh_loaded[1], 16)

            def turn(i):
                for u in range(RING):
                    make_scatter(i * RING + u + LEAD, (u + LEAD) % 4, u % 2, i * RING + u + LEAD + RING - 3)
                    add_window(i * RING + u - HALF, u % HALF, 1 - u // HALF, i * 2 + u // HALF + 2)

            with dve.Fori(1, CHECK_TURN) as i:
                turn(i)
            n = done(dve.tensor_scalar(outside[:, :], rel[:, :], 0.0, None, ALU.is_lt))
            dve.wait_ge(chain, n)
            n = done(dve.scalar_tensor_tensor(out=outside[:, :], in0=rel[:, :], scalar=float(W), in1=outside[:, :],
                                              op0=ALU.is_ge, op1=ALU.max))
            dve.wait_ge(chain, n)
            dve.tensor_reduce(group_out[:, :], outside[:, :].rearrange("p (g t) -> p g t", t=TPG), AX_X, ALU.max
                              ).then_inc(outside_ready, 1)
            dve.wait_ge(outside_counted, 1)
            done(dve.tensor_reduce(n_out_f[:, :], fin[0][0:1, 0:GROUPS], AX_X, ALU.add))
            dve.tensor_copy(n_out[:, :], fin[0][0:1, 0:GROUPS]).then_inc(counts_ready, 1)
            dve.wait_ge(chain, done(dve.tensor_tensor(falls[:, 0:GROUPS - 1], base_f[:, 1:GROUPS],
                                                      base_f[:, 0:GROUPS - 1], ALU.is_lt)))
            at = EARLY_TURN * RING - HALF
            done(dve.tensor_scalar(late[:, :], base_f[:, at:at + 1], float(EARLY * P), None, ALU.is_lt))
            dve.wait_ge(chain, done(dve.tensor_reduce(n_falls[:, :], falls[:, 0:GROUPS - 1], AX_X, ALU.add)))
            n = done(dve.scalar_tensor_tensor(out=held_f[:, :], in0=late[:, :], scalar=n_falls[:, 0:1],
                                              in1=n_out_f[:, :], op0=ALU.add, op1=ALU.add))
            dve.wait_ge(chain, n)
            dve.tensor_copy(held[:, :], held_f[:, :]).then_inc(counts_ready, 1)
            dve.tensor_copy(n_out_all[:, :], n_out_f[:, :]).then_inc(counts_ready, 1)
            for c in range(CHUNKS - H_BUFS, CHUNKS):
                add_h(c)

            left = edges_left(dve)
            hold = early_held(dve)

            def finish(first, last):
                for n, j, e in finish_steps(first, last):
                    dve.wait_ge(turned, n + 1)
                    dve.scalar_tensor_tensor(out=xh[:, j:e, :], in0=fin[n % FIN_BANKS][:, 0:(e - j) * D].rearrange(
                        "p (j d) -> p j d", d=D), scalar=0.0, in1=xh[:, j:e, :], op0=ALU.max, op1=ALU.add
                    ).then_inc(finished, 1)

            with dve.Fori(CHECK_TURN, EARLY_TURN) as i:
                turn(i)
            with dve.If(hold == 0):
                dve.wait_ge(added, 2 * (EARLY_TURN * RING - HALF) + 4 * HALF)
                dve.sem_inc(sums_ready, 1)
                finish(0, EARLY)
            with dve.Fori(EARLY_TURN, TURNS) as i:
                turn(i)
            for g in range(TURNS * RING + LEAD, GROUPS):
                make_scatter(g, g % 4, g % 2, g + RING - 3)
            last_bases = {g: first_node(g) for g in range(TURNS * RING, GROUPS)}
            for g in range(TURNS * RING - HALF, GROUPS):
                add_window(g, g % HALF, g // HALF % 2, g // HALF + 3, last_bases.get(g))
            dve.wait_ge(added, 2 * GROUPS + 4 * HALF)
            with dve.If(left > 0):
                dve.tensor_copy(rel[:, :], dst_i[:, :]).then_inc(left_dst, 1)
                dve.wait_ge(left_dst, 1)
                dve.scalar_tensor_tensor(out=rel[:, :], in0=rel[:, :], scalar=1.0, in1=outside[:, :],
                                         op0=ALU.add, op1=ALU.mult).then_inc(left_dst, 1)
                dve.wait_ge(left_dst, 2)
                dve.tensor_scalar(rel[:, :], rel[:, :], -1.0, None, ALU.add).then_inc(left_dst, 1)
                dve.wait_ge(left_dst, 3)
                with dve.Fori(0, GROUPS) as g:
                    with dve.If(group_left(dve, g) > 0):
                        with dve.Fori(0, WINDOWS) as j:
                            dve.tensor_tensor(onehot[:, 0, :, :],
                                              iota_w[:, :].unsqueeze(1).to_broadcast([P, TPG, W]),
                                              rel[:, bass.ds(g * TPG, TPG)].unsqueeze(2).to_broadcast([P, TPG, W]),
                                              ALU.is_equal).then_inc(left_onehot, 1)
                            dve.wait_ge(left_onehot, 1)
                            dve.sem_inc(left_onehot, -1)
                            dve.tensor_tensor(
                                scat[:, 0, :, :, :], onehot[:, 0, :, :].unsqueeze(2).to_broadcast([P, TPG, 4, W]),
                                sh_sb[:, bass.ds(g * TPG, TPG), :].unsqueeze(3).to_broadcast([P, TPG, 4, W]),
                                ALU.mult).then_inc(left_scat, 1)
                            dve.tensor_scalar(rel[:, bass.ds(g * TPG, TPG)], rel[:, bass.ds(g * TPG, TPG)],
                                              -float(W), None, ALU.add).then_inc(left_added, 1)
                            dve.wait_ge(left_mapped, 1)
                            dve.sem_inc(left_mapped, -1)
                            here = bass.ds(j * W, W)
                            dve.tensor_tensor(acc1[:, here], acc1[:, here], pB1[0][:, 0:W], ALU.add
                                              ).then_inc(left_added, 1)
                            dve.tensor_tensor(acc2[:, here], acc2[:, here], pB2[0][0:F2, 0:W], ALU.add
                                              ).then_inc(left_added, 1)
                            dve.wait_ge(left_added, 3)
                            dve.sem_inc(left_added, -3)
            dve.sem_inc(sums_ready, 1)

            with dve.If(hold > 0):
                dve.sem_inc(sums_ready, 1)
                finish(0, EARLY)
            finish(EARLY, BLOCKS)

        @block.tensor
        def _(pe):
            pe.sem_inc(agg_done, RING)
            pe.sem_inc(mapped, 2)
            pe.sem_inc(agg_copied, 2)
            pe.wait_ge(z_ready, 16)
            for blk in range(4):
                kk, w = (MUL0, ws_s) if blk == 0 else (MUL1, wv_s)
                cols = slice(0, MUL0) if blk == 0 else slice(MUL0 + blk - 1, D, 3)
                for k in range(4):
                    nc.tensor.matmul(fin[k][:, cols], z[0:kk, blk, k, 0:F1], w[:, :], start=True, stop=True)
                    last = nc.tensor.matmul(pB[1][F2 * k:F2 * k + F2, cols], z[0:kk, blk, k, F1:D], w[:, :],
                                            start=True, stop=True, tile_position=(0, F2 * k))
            last.then_inc(L_product, 1)
            pe.wait_ge(base_ready, 2)
            nc.tensor.matmul(pA[0][:, 0:GROUPS], ones_row[:, :], base_f[:, :], start=True, stop=True
                             ).then_inc(base_spread, 1)
            pe.wait_ge(base_spread, 2)

            def sum_window(slot, s, b, m):
                nodes = slice(m * W, (m + 1) * W)
                for t in range(TPG):
                    nc.tensor.matmul(half_view(pA1[b])[:, :, nodes], rows[:, slot, t, 0:F1], scat[:, s, t, :, :],
                                     start=(t == 0), stop=(t == TPG - 1))
                for t in range(TPG):
                    for k in range(4):
                        last = nc.tensor.matmul(pA2[b][F2 * k:F2 * k + F2, nodes], rows[:, slot, t, F1:D],
                                                scat[:, s, t, k, :], start=(t == 0), stop=(t == TPG - 1),
                                                tile_position=(0, F2 * k))
                return last

            def map_sums(b, n):
                for o, cols in ((pB1[b][:, 0:n], slice(0, F1)), (pB2[b][0:F2, 0:n], slice(F1, D))):
                    for k in range(4):
                        nc.tensor.matmul(o, L1[:, k, cols], agg1[:, b, k, 0:n], start=(k == 0), stop=False)
                    last = nc.tensor.matmul(o, L2[:, cols], agg2[:, b, 0:n], start=False, stop=True)
                return last

            def aggregate(slot, landed, scattered, by=None):
                pe.wait_ge(by if by is not None else gathered[slot], landed)
                pe.wait_ge(scat_ready, scattered)
                pe.sem_inc(slot_seen_free, 1)
                sum_window(slot, slot % 4, slot // HALF, slot % HALF).then_inc(agg_done, 1)

            def map_half(b, copied, free, groups=HALF):
                pe.wait_ge(agg_copied, copied)
                pe.wait_ge(added, free)
                pe.sem_inc(slot_seen_free, 1)
                map_sums(b, groups * W).then_inc(mapped, 1)

            for g in range(RING):
                aggregate(g, g * TPG + TPG, g + 1, rows_normed)
                if g == HALF:
                    pe.wait_ge(L_ready, 5)
                    map_half(0, 4, 2 * HALF)

            def turn(i):
                for u in range(RING):
                    if u % HALF == 0:
                        pe.wait_ge(agg_copied, i * 4 + u // HALF * 2)
                        pe.sem_inc(slot_seen_free, 1)
                    aggregate(u, i * (16 * TPG) + 16 * TPG, i * RING + u + 1)
                    if u % HALF == 0:
                        map_half(1 - u // HALF, i * 4 + u // HALF * 2 + 2,
                                 i * (4 * HALF) + u // HALF * (2 * HALF))

            with pe.Fori(1, CHECK_TURN) as i:
                turn(i)
            pe.wait_ge(outside_ready, 1)
            nc.tensor.matmul(fin[0][0:1, 0:GROUPS], ones_col[:, :], group_out[:, :], start=True, stop=True
                             ).then_inc(outside_counted, 1)
            left = edges_left(pe)
            hold = early_held(pe)

            def turn_blocks(first, last):
                for n, j, e in finish_steps(first, last):
                    if n >= FIN_BANKS:
                        pe.wait_ge(finished, n - FIN_BANKS + 1)
                    for q in range(j, e):
                        o = fin[n % FIN_BANKS][:, (q - j) * D:(q - j + 1) * D]
                        nc.tensor.transpose(o[:, 0:F1], acc1[:, q * P:(q + 1) * P], ident[:, :])
                        last_one = nc.tensor.transpose(o[:, F1:D], acc2[:, q * P:(q + 1) * P], ident[0:F2, 0:F2])
                    last_one.then_inc(turned, 1)

            with pe.Fori(CHECK_TURN, EARLY_TURN) as i:
                turn(i)
            pe.wait_ge(const_made, 3)
            with pe.If(hold == 0):
                pe.wait_ge(sums_ready, 1)
                turn_blocks(0, EARLY)
            with pe.Fori(EARLY_TURN, TURNS) as i:
                turn(i)
            pe.wait_ge(agg_copied, 2 * LAST_HALF)
            for u in range(TAIL):
                aggregate(u, (TURNS + 1) * 16 * TPG, TURNS * RING + u + 1)
                if u == 0:
                    map_half(1, 2 * LAST_HALF + 2, 2 * HALF * LAST_HALF)
            map_half(0, 2 * LAST_HALF + 4, 2 * HALF * (LAST_HALF + 1), TAIL)
            with pe.If(left > 0):
                pe.wait_ge(added, 2 * GROUPS + 4 * HALF)
                pe.sem_inc(left_group_done, 1)
                with pe.Fori(0, GROUPS) as g:
                    pe.wait_ge(left_rows, g * (16 * TPG) + 16 * TPG)
                    with pe.If(group_left(pe, g) > 0):
                        with pe.Fori(0, WINDOWS) as _j:
                            pe.wait_ge(left_scat, 1)
                            pe.sem_inc(left_scat, -1)
                            sum_window(0, 0, 0, 0).then_inc(left_agg, 1)
                            pe.wait_ge(left_copied, 2)
                            pe.sem_inc(left_copied, -2)
                            map_sums(0, W).then_inc(left_mapped, 1)
                    pe.sem_inc(left_group_done, 1)

            pe.wait_ge(sums_ready, 2)
            with pe.If(hold > 0):
                turn_blocks(0, EARLY)
            turn_blocks(EARLY, BLOCKS)


_INS = ["x", "src", "dst", "sh", "w1t", "w2t", "w3t", "w4t", "w5t", "ws", "wv"]


def kernel(x, src, dst, edge_attr_4, L0_gnn_W1, L0_gnn_W2, L0_gnn_W3, L0_gnn_W4, L0_gnn_W5, L0_gnn_Ws, L0_gnn_Wv):
    import numpy as _np
    import concourse.bacc as _bacc
    from concourse import mybir as _mybir
    from concourse.bass_utils import run_bass_kernel_spmd as _run

    pad = TILES * P - EDGES
    src_t = _np.pad(_np.asarray(src), (0, pad), mode="edge").reshape(TILES, P).T
    dst_t = _np.pad(_np.asarray(dst), (0, pad), mode="edge").reshape(TILES, P).T
    sh_t = _np.pad(_np.asarray(edge_attr_4), ((0, pad), (0, 0))).reshape(TILES, P, 4).transpose(1, 0, 2).reshape(
        P, TILES * 4)
    values = [x, src_t, dst_t, sh_t, _np.asarray(L0_gnn_W1).T, _np.asarray(L0_gnn_W2).T, _np.asarray(L0_gnn_W3).T,
              _np.asarray(L0_gnn_W4).T, _np.asarray(L0_gnn_W5).T, L0_gnn_Ws, L0_gnn_Wv]

    nc = _bacc.Bacc("TRN2", target_bir_lowering=False, num_devices=1)
    arrays, args = {}, []
    for name, value in zip(_INS, values):
        a = _np.ascontiguousarray(value)
        arrays[f"in_{name}_dram"] = a
        args.append(nc.dram_tensor(f"in_{name}_dram", a.shape, _mybir.dt.from_np(a.dtype), kind="ExternalInput").ap())
    args.append(nc.dram_tensor("table_dram", (NODES, D), F32, kind="Internal").ap())
    args.append(nc.dram_tensor("out_0_dram", (NODES, D), F32, kind="ExternalOutput").ap())
    gnn_kernel(nc, *args)
    r = _run(nc, [arrays], core_ids=[0])
    return r.results[0]["out_0_dram"]
```
